# Optimizing a Trainium2 kernel written in Bass

```python
import numpy as np
import jax
import jax.numpy as jnp

def _softmax(x, axis=-1):
    return jax.nn.softmax(x, axis=axis)
def _gelu(x):
    return jax.nn.gelu(x, approximate=True)
def _silu(x):
    return jax.nn.silu(x)
def _sigmoid(x):
    return jax.nn.sigmoid(x)
def _layernorm(x, axis=-1, eps=1e-5):
    m = jnp.mean(x, axis=axis, keepdims=True)
    v = jnp.var(x, axis=axis, keepdims=True)
    return (x - m) / jnp.sqrt(v + eps)
def _scatter_add(tgt, idx, src, axis=0):
    return tgt.at[idx].add(src)
def _segment_sum(src, seg, n):
    return jax.ops.segment_sum(src, seg, n)

kernel_name = 'mk_adj_resnorm_d4_adj_512_1c36ef'

def setup_inputs(seed: int = 0):
    np.random.seed(seed)
    _w = jnp.asarray
    def _rec_inputs():
        import jax
        import jax.numpy as jnp
        _gk = jax.random.key(seed)
        x = -0.001547 + 1.001 * jax.random.normal(jax.random.fold_in(_gk, 1), (128, 128, 512), jnp.float32)
        _a = jax.random.bernoulli(jax.random.fold_in(_gk, 2), 0.03125, (128, 128))
        _a = jnp.logical_or(_a, jnp.swapaxes(_a, -1, -2))
        _a = jnp.logical_or(_a, jnp.eye(128, dtype=bool))
        _af = _a.astype(jnp.float32)
        _af = _af * jax.random.uniform(jax.random.fold_in(_gk, 3), (128, 128), jnp.float32, 0.05, 0.237401)
        adj = _af
        return x, adj
    x, adj = _rec_inputs()
    def _L0_gnn_setup():
        import jax, jax.numpy as jnp
        import numpy as np
        key = jax.random.key(seed)
        k1, k2, k3, k4 = jax.random.split(key, 4)
        B, D, N = (4, 128, 512)
        scale = 1.0 / np.sqrt(2 * D)
        x = jax.random.normal(k1, (B, D, N), dtype=jnp.float32)
        W1 = jax.random.normal(k2, (D, D), dtype=jnp.float32) * scale
        W2 = jax.random.normal(k3, (D, D), dtype=jnp.float32) * scale
        b = jax.random.normal(k4, (D,), dtype=jnp.float32) * scale
        return {'x': x, 'W1': W1, 'W2': W2, 'b': b}
    _L0_gnn_all = _L0_gnn_setup()
    _L0_gnn_in = {k: v for k, v in _L0_gnn_all.items() if k in ('b', )}
    del _L0_gnn_all

    def _L1_gnn_setup():
        import jax, jax.numpy as jnp
        import numpy as np
        ALPHA = 0.2
        key = jax.random.key(seed)
        k0, k1, k2, k3 = jax.random.split(key, 4)
        B, N, C, F = (64, 1024, 512, 512)
        x = jax.random.normal(k0, (B, N, C), dtype=jnp.float32)
        W = jax.random.normal(k1, (C, F), dtype=jnp.float32) * (1.414 / np.sqrt(C + F))
        a = jax.random.normal(k2, (2 * F, 1), dtype=jnp.float32) * (1.414 / np.sqrt(2 * F + 1))
        beta = jnp.ones((1,), dtype=jnp.float32)
        mask = (jax.random.uniform(k3, (N, N)) < 0.3).astype(jnp.float32)
        return {'x': x, 'W': W, 'a': a, 'beta': beta, 'mask': mask}
    _L1_gnn_all = _L1_gnn_setup()
    _L1_gnn_in = {k: v for k, v in _L1_gnn_all.items() if k in ('W', 'a', 'beta', )}
    del _L1_gnn_all

    def _L2_gnn_setup():
        import jax, jax.numpy as jnp
        import numpy as np
        B, N, D, O = (8, 4096, 512, 512)
        key = jax.random.key(seed)
        k1, k2, k3, k4 = jax.random.split(key, 4)
        x = jax.random.normal(k1, (B, N, D), dtype=jnp.float32)
        adj = jax.random.uniform(k2, (N, N), dtype=jnp.float32)
        weight = jax.random.normal(k3, (D, O), dtype=jnp.float32) * 0.02
        bias = jax.random.normal(k4, (O,), dtype=jnp.float32) * 0.02
        return {'x': x, 'adj': adj, 'weight': weight, 'bias': bias}
    _L2_gnn_all = _L2_gnn_setup()
    _L2_gnn_in = {k: v for k, v in _L2_gnn_all.items() if k in ('weight', 'bias', )}
    del _L2_gnn_all

    def _L3_gnn_setup():
        import jax, jax.numpy as jnp
        import numpy as np
        B, N, D = (4, 2048, 512)
        H, HD = (8, 64)
        key = jax.random.key(seed)
        ks = jax.random.split(key, 6)
        x = jax.random.normal(ks[0], (B, N, D), dtype=jnp.float32)
        adj = (jax.random.uniform(ks[1], (N, N)) < 0.1).astype(jnp.float32)
        adj = jnp.maximum(adj, jnp.eye(N, dtype=jnp.float32))
        s = 0.02
        Wq = jax.random.normal(ks[2], (D, H * HD), dtype=jnp.float32) * s
        Wk = jax.random.normal(ks[3], (D, H * HD), dtype=jnp.float32) * s
        Wv = jax.random.normal(ks[4], (D, H * HD), dtype=jnp.float32) * s
        bq = jnp.zeros((H * HD,), dtype=jnp.float32)
        bk = jnp.zeros((H * HD,), dtype=jnp.float32)
        bv = jnp.zeros((H * HD,), dtype=jnp.float32)
        return {'x': x, 'adj': adj, 'Wq': Wq, 'bq': bq, 'Wk': Wk, 'bk': bk, 'Wv': Wv, 'bv': bv}
    _L3_gnn_all = _L3_gnn_setup()
    _L3_gnn_in = {k: v for k, v in _L3_gnn_all.items() if k in ('Wq', 'bq', 'Wk', 'bk', 'Wv', 'bv', )}
    del _L3_gnn_all

    return {
        "x": x,
        "adj": adj,
        "L0_gnn_b": _L0_gnn_in["b"],
        "L1_gnn_W": _L1_gnn_in["W"],
        "L1_gnn_a": _L1_gnn_in["a"],
        "L1_gnn_beta": _L1_gnn_in["beta"],
        "L2_gnn_weight": _L2_gnn_in["weight"],
        "L2_gnn_bias": _L2_gnn_in["bias"],
        "L3_gnn_Wq": _L3_gnn_in["Wq"],
        "L3_gnn_bq": _L3_gnn_in["bq"],
        "L3_gnn_Wk": _L3_gnn_in["Wk"],
        "L3_gnn_bk": _L3_gnn_in["bk"],
        "L3_gnn_Wv": _L3_gnn_in["Wv"],
        "L3_gnn_bv": _L3_gnn_in["bv"],
    }

def reference(x, adj, L0_gnn_b, L1_gnn_W, L1_gnn_a, L1_gnn_beta, L2_gnn_weight, L2_gnn_bias, L3_gnn_Wq, L3_gnn_bq, L3_gnn_Wk, L3_gnn_bk, L3_gnn_Wv, L3_gnn_bv):
    import jax
    import jax.numpy as jnp
    def _L0_gnn_ref(x, W1, W2, b):
        import jax, jax.numpy as jnp
        import numpy as np
        A = jnp.einsum('od,bdn->bon', W1, x)
        C = jnp.einsum('od,bdn->bon', W2, x) + b[None, :, None]
        pre = A[:, :, None, :] + (C - A)[:, :, :, None]
        out = jnp.max(jax.nn.relu(pre), axis=-1)
        return out

    def _L1_gnn_ref(x, W, a, beta, mask):
        import jax, jax.numpy as jnp
        import numpy as np
        ALPHA = 0.2
        F_ = W.shape[1]
        h = jnp.einsum('bnc,cf->bnf', x, W)
        a1, a2 = (a[:F_, 0], a[F_:, 0])
        s1 = jnp.einsum('bnf,f->bn', h, a1)
        s2 = jnp.einsum('bnf,f->bn', h, a2)
        e = jax.nn.leaky_relu(s1[:, :, None] + s2[:, None, :], negative_slope=ALPHA)
        e = e * mask[None, :, :]
        att = jax.nn.softmax(e, axis=2)
        h_prime = jnp.einsum('bij,bjf->bif', att, h)
        return jax.nn.elu(h_prime + beta * h)

    def _L2_gnn_ref(x, adj, weight, bias):
        import jax, jax.numpy as jnp
        import numpy as np
        B, N, D, O = (8, 4096, 512, 512)
        y = jnp.einsum('nm,bmd->bnd', adj, x)
        out = jnp.einsum('bnd,do->bno', y, weight) + bias
        return out

    def _L3_gnn_ref(x, adj, Wq, bq, Wk, bk, Wv, bv):
        import jax, jax.numpy as jnp
        import numpy as np
        B, N, D = (4, 2048, 512)
        H, HD = (8, 64)
        b, n, _ = x.shape
        q = (x @ Wq + bq).reshape(b, n, H, HD)
        k = (x @ Wk + bk).reshape(b, n, H, HD)
        v = (x @ Wv + bv).reshape(b, n, H, HD)
        scores = jnp.einsum('bihd,bjhd->bhij', q, k) / jnp.sqrt(jnp.float32(HD))
        mask = jnp.where(adj == 0, jnp.float32(-1000000000.0), jnp.float32(0.0))
        scores = scores + mask[None, None, :, :]
        weights = jax.nn.softmax(scores, axis=-1)
        out = jnp.einsum('bhij,bjhd->bihd', weights, v)
        return out.reshape(b, n, H * HD)

    x = _layernorm(x + _L0_gnn_ref(x, adj, adj, L0_gnn_b), axis=-1)
    x = _layernorm(x + _L1_gnn_ref(x, L1_gnn_W, L1_gnn_a, L1_gnn_beta, adj), axis=-1)
    x = _layernorm(x + _L2_gnn_ref(x, adj, L2_gnn_weight, L2_gnn_bias), axis=-1)
    x = _layernorm(x + _L3_gnn_ref(x, adj, L3_gnn_Wq, L3_gnn_bq, L3_gnn_Wk, L3_gnn_bk, L3_gnn_Wv, L3_gnn_bv), axis=-1)
    return x


_drawn_inputs = setup_inputs


def setup_inputs(seed=0):
    import zlib

    import numpy as np

    out = dict(_drawn_inputs(seed))
    spreads = {'L3_gnn_bq': (0.0, 0.8), 'L3_gnn_bk': (0.0, 0.8), 'L3_gnn_bv': (0.0, 0.1)}
    factors = {'L0_gnn_b': 8.0, 'L1_gnn_a': 8.0, 'L2_gnn_bias': 2.855}
    for name, (base, spread) in spreads.items():
        noise = np.random.default_rng([zlib.crc32(name.encode()), seed]).standard_normal(out[name].shape)
        drawn = base * np.exp(spread * noise) if base else spread * noise
        out[name] = jnp.asarray(drawn.astype(out[name].dtype))
    for name, factor in factors.items():
        out[name] = (out[name] * factor).astype(out[name].dtype)
    return out
```

```python
from contextlib import ExitStack

import concourse.bass as bass
from concourse import mybir

F32 = mybir.dt.float32
F32R = mybir.dt.float32r
ALU = mybir.AluOpType
ACT = mybir.ActivationFunctionType
AX = mybir.AxisListType

GRAPHS, NODES, FEATS = 128, 128, 512
P = 128
KC = FEATS // P
HEAD = 64
GROUP = 2
BUFS = 2 * GROUP
CHUNKS = KC // GROUP
TILES = CHUNKS * GROUP
EPS = 1e-5
SLOPE = 0.2
SCALE = 1.0 / 8.0
MASKED = -1.0e9 / SCALE

L_LOAD = -3
L_EDGE = 0
L_ATT = 1
L_GAT = 2
L_GCN = 3
L_TR = 4
L_V = 5
L_QK = GROUP + 4
L_PV = L_QK + 1
WARM = -(-(L_PV + 2) // BUFS) * BUFS
LOOP_END = WARM + (GRAPHS + L_LOAD - WARM) // BUFS * BUFS
SLOTS = GRAPHS + L_PV


class Slot:

    def __init__(self, base, offset):
        self.base, self.offset = base, offset

    def on(self, lag):
        return not isinstance(self.base, int) or 0 <= self.base + self.offset - lag < GRAPHS

    def first(self, lag):
        return isinstance(self.base, int) and self.base + self.offset == lag

    def graph(self, lag):
        return self.base + (self.offset - lag)

    def buf(self, lag, count):
        return (self.offset - lag) % count

    def part(self, lag):
        return (self.offset - lag) % GROUP

    def wait(self, eng, sem, lag, ago=0):
        value = self.base + (self.offset - lag - ago + 1)
        if not isinstance(self.base, int):
            eng.wait_ge(sem, value)
        elif min(value, GRAPHS) > 0:
            eng.wait_ge(sem, min(value, GRAPHS))

    def wait_last(self, eng, *jobs):
        for sem, lag, ago in jobs:
            if Slot(self.base, self.offset - ago).on(lag):
                Slot(self.base, self.offset - ago).wait(eng, sem, lag)
                return


def slots(eng, emit):
    for s in range(WARM):
        emit(Slot(s - s % BUFS, s % BUFS))
    with eng.Fori(0, (LOOP_END - WARM) // BUFS) as turn:
        for c in range(BUFS):
            emit(Slot(turn * BUFS + WARM, c))
    for s in range(LOOP_END, SLOTS):
        emit(Slot(s - s % BUFS, s % BUFS))


def graph_layers_kernel(nc, x, adj, l0_b, l1_w, l1_a, l1_beta, l2_w, l2_bias,
                        wq, bq, wk, bk, wv, bv, out):
    ctx = ExitStack()
    with ctx:
        def sb(name, shape, dt=F32):
            return ctx.enter_context(nc.sbuf_tensor(name, shape, dt))

        def sem(name):
            return ctx.enter_context(nc.semaphore(name))

        weights = {n: (sb(f"{n}_hi", [P, KC, FEATS], F32R), sb(f"{n}_lo", [P, KC, FEATS], F32R))
                   for n in ("w1", "w2", "wq", "wk", "wv")}
        adj_sb = sb("adj_sb", [P, P])
        adj_t = sb("adj_t", [P, P])
        adj_t_hi, adj_t_lo = sb("adj_t_hi", [P, P], F32R), sb("adj_t_lo", [P, P], F32R)
        ident = sb("ident", [P, P])
        beta_i = sb("beta_i", [P, P])
        mask = sb("mask", [P, P])
        b0_col = sb("b0_col", [P, 1])
        beta_col = sb("beta_col", [P, 1])
        a_col = sb("a_col", [P, 2 * KC])
        qb_col = sb("qb_col", [P, KC])
        kb_col = sb("kb_col", [P, KC])
        half_neg = sb("half_neg", [P, 1])
        eps_col = sb("eps_col", [P, 1])
        u1 = sb("u1", [P, FEATS])
        u2 = sb("u2", [P, FEATS])
        bias2 = sb("bias2", [P, FEATS])
        bv_row = sb("bv_row", [P, FEATS])

        x_in = sb("x_in", [P, 4, FEATS])
        x_hi, x_lo = sb("x_hi", [P, FEATS], F32R), sb("x_lo", [P, FEATS], F32R)
        x1 = sb("x1", [P, 4, FEATS])
        x2 = sb("x2", [P, 2, FEATS])
        x2b = sb("x2b", [P, FEATS])
        x3 = sb("x3", [P, 2, FEATS])
        x4 = sb("x4", [P, BUFS, FEATS])
        e1 = sb("e1", [P, FEATS])
        r1 = sb("r1", [P, 2, FEATS])
        r2 = sb("r2", [P, FEATS])
        y1_hi, y1_lo = sb("y1_hi", [P, FEATS], F32R), sb("y1_lo", [P, FEATS], F32R)
        y2_hi, y2_lo = sb("y2_hi", [P, FEATS], F32R), sb("y2_lo", [P, FEATS], F32R)
        xt_hi = sb("xt_hi", [P, KC, BUFS, P], F32R)
        xt_lo = sb("xt_lo", [P, KC, BUFS, P], F32R)
        q_sb = sb("q_sb", [P, CHUNKS, GROUP * P])
        k_sb = sb("k_sb", [P, CHUNKS, GROUP * P])
        v_sb = sb("v_sb", [P, BUFS, FEATS])
        s_masked = sb("s_masked", [P, 2, TILES, P])
        probs = sb("probs", [P, 2, 2, TILES, P])
        probs_t = sb("probs_t", [P, 2, TILES, P])
        o_norm = sb("o_norm", [P, GROUP, CHUNKS * P])
        out_sb = sb("out_sb", [P, GROUP, FEATS])

        z0 = sb("z0", [P, 2, P])
        lrelu = sb("lrelu", [P, 2, P])
        att_e = sb("att_e", [P, 2, P])
        att_p = sb("att_p", [P, 2, P])
        att_n = sb("att_n", [P, 2, P])
        att_t = sb("att_t", [P, 2, P])
        dot_tmp = sb("dot_tmp", [P, 2, FEATS])
        s1_col = sb("s1_col", [P, 4])
        s2_col = sb("s2_col", [P, 4])
        att_max = sb("att_max", [P, 2])
        att_nmax = sb("att_nmax", [P, 2])
        att_sum = sb("att_sum", [P, 2])
        att_inv = sb("att_inv", [P, 2])
        edge_max = sb("edge_max", [P, 1])
        edge_c = sb("edge_c", [P, 1])
        edge_m = sb("edge_m", [P, 1])
        edge_d = sb("edge_d", [P, 1])
        st = {n: sb(f"st_{n}", [P, 6 * k]) for n, k in (("0", 1), ("1", 1), ("2", 1), ("3", GROUP))}
        mv = {n: sb(f"mv_{n}", [P, 2, 2 * k]) for n, k in (("0", 1), ("1", 1), ("2", 1), ("3", GROUP))}
        ve = {n: sb(f"ve_{n}", [P, k]) for n, k in (("0", 1), ("1", 1), ("2", 1), ("3", GROUP))}
        rs = {n: sb(f"rs_{n}", [P, 2, k]) for n, k in (("0", 1), ("1", 1), ("2", 1), ("3", GROUP))}
        sc_max = sb("sc_max", [P, 2, TILES])
        sc_nmax = sb("sc_nmax", [P, 2, TILES])
        sc_sum = sb("sc_sum", [P, 2, 2 * TILES])
        sc_inv = sb("sc_inv", [P, 2 * TILES])

        rot = [ctx.enter_context(nc.psum_tensor(f"rot{n}", [P, 512], F32)) for n in range(4)]
        score_bank = [ctx.enter_context(nc.psum_tensor(f"score{n}", [P, 512], F32)) for n in range(2)]
        s2_bank = ctx.enter_context(nc.psum_tensor("s2_bank", [P, 512], F32))
        att_bank = ctx.enter_context(nc.psum_tensor("att_bank", [P, 512], F32))

        stage = [probs[:, :, :, :, :].rearrange("p a b t n -> p (a b t n)").rearrange("p (k n) -> p k n", k=KC),
                 v_sb[:, :, :]]
        w_t = x4[:, :, :]

        const_in = sem("const_in")
        w_in = [sem(f"w_in{n}") for n in range(2)]
        w_hi_done, w_lo_done = sem("w_hi_done"), sem("w_lo_done")
        adj_hi_done, x_hi_done, x_lo_done = sem("adj_hi_done"), sem("x_hi_done"), sem("x_lo_done")
        ident_zero, ident_done, consts_done = sem("ident_zero"), sem("ident_done"), sem("consts_done")
        setup_mm, setup_copied = sem("setup_mm"), sem("setup_copied")
        x_loaded = [sem(f"x_loaded{n}") for n in range(4)]
        out_stored = [sem(f"out_stored{n}") for n in range(GROUP)]
        (s2_mm, q_mm, y1_mm, k_mm, pt0_mm, pt1_mm, att_t_mm, z1_mm, y2_mm, pv_mm, edge_mm, score_mm,
         z2_mm, xt_mm, v_mm) = (sem(n) for n in (
            "s2_mm", "q_mm", "y1_mm", "k_mm", "pt0_mm", "pt1_mm", "att_t_mm", "z1_mm", "y2_mm",
            "pv_mm", "edge_mm", "score_mm", "z2_mm", "xt_mm", "v_mm"))
        (z0_done, q_done, y1_hi_done, att_exp, k_done, pt0_done, att_t_done, e1_done,
         y2_hi_done, score_exp, xt_hi_done, v_done) = (sem(n) for n in (
            "z0_done", "q_done", "y1_hi_done", "att_exp", "k_done", "pt0_done", "att_t_done",
            "e1_done", "y2_hi_done", "score_exp", "xt_hi_done", "v_done"))
        (lrelu_done, att_max_done, att_nmax_done, y1_lo_done, att_inv_done, att_n_done,
         pt1_done, r1_done, y2_lo_done, o_norm_done, inv_done, edge_max_done, edge_c_done,
         edge_m_done, edge_d_done, masked_done, score_max_done, score_nmax_done, x1_done, dots_done,
         x2_done, r2_done, xt_lo_done, x3_done, out_done) = (sem(n) for n in (
            "lrelu_done", "att_max_done", "att_nmax_done", "y1_lo_done",
            "att_inv_done", "att_n_done", "pt1_done", "r1_done", "y2_lo_done",
            "o_norm_done", "inv_done", "edge_max_done", "edge_c_done", "edge_m_done", "edge_d_done",
            "masked_done", "score_max_done", "score_nmax_done", "x1_done", "dots_done", "x2_done",
            "r2_done", "xt_lo_done", "x3_done", "out_done"))
        st_done = {n: sem(f"st_done{n}") for n in "0123"}
        mv_done = {n: sem(f"mv_done{n}") for n in "0123"}
        ve_done = {n: sem(f"ve_done{n}") for n in "0123"}
        rs_done = {n: sem(f"rs_done{n}") for n in "0123"}
        (e1m_done, r1_sum_done, x2b_done, x4_init, x4_done) = (sem(n) for n in (
            "e1m_done", "r1_sum_done", "x2b_done", "x4_init", "x4_done"))

        w_order = ["w1", "w2", "wv", "wq", "wk"]
        w_dram = {"w1": l1_w, "w2": l2_w, "wq": wq, "wk": wk, "wv": wv}
        N_CONST = 10

        block = ctx.enter_context(nc.Block())

        @block.sync
        def _(sp):
            def load(graph, buf):
                sp.dma_start(x_in[:, buf, :], x[bass.ds(graph, 1), :, :].rearrange("b i c -> i (b c)"))\
                  .then_inc(x_loaded[buf], 16)

            for n in range(2):
                sp.dma_start(stage[n], w_dram[w_order[n]].rearrange("(k p) n -> p k n", p=P))\
                  .then_inc(w_in[n], 16)
            for dst, src in ((adj_sb[:, :], adj),
                             (b0_col[:, :], l0_b.rearrange("(p o) -> p o", o=1)),
                             (beta_col[:, :], l1_beta.rearrange("(p o) -> p o", o=1).to_broadcast([P, 1])),
                             (a_col[:, :], l1_a.rearrange("(k p) o -> p (k o)", p=P)),
                             (qb_col[:, :], bq.rearrange("(k p) -> p k", p=P)),
                             (kb_col[:, :], bk.rearrange("(k p) -> p k", p=P)),
                             (bias2[:, :], l2_bias.rearrange("(o n) -> o n", o=1).to_broadcast([P, FEATS])),
                             (bv_row[:, :], bv.rearrange("(o n) -> o n", o=1).to_broadcast([P, FEATS]))):
                sp.dma_start(dst, src, allow_slow_non_contiguous=True).then_inc(const_in, 16)
            for n in range(-L_LOAD):
                load(n, n % 4)

            def emit(slot):
                if slot.on(L_LOAD):
                    buf = slot.buf(L_LOAD, 4)
                    slot.wait(sp, x_lo_done, L_LOAD, 4)
                    slot.wait(sp, x1_done, L_LOAD, 4)
                    load(slot.graph(L_LOAD), buf)
                for n in range(2, len(w_order)):
                    if slot.first(n - 2):
                        sp.wait_ge(w_lo_done, n - 1)
                        if n == 2:
                            sp.wait_ge(setup_mm, 2)
                        sp.dma_start(stage[n % 2], w_dram[w_order[n]].rearrange("(k p) n -> p k n", p=P))\
                          .then_inc(w_in[n % 2], 16)
                if slot.on(L_PV) and slot.part(L_PV) == GROUP - 1:
                    slot.wait(sp, out_done, L_PV)
                    for g in range(GROUP):
                        sp.dma_start(out[bass.ds(slot.graph(L_PV + GROUP - 1 - g), 1), :, :].rearrange("b i c -> i (b c)"),
                                     out_sb[:, g, :]).then_inc(out_stored[g], 16)

            slots(sp, emit)
            for g in range(GROUP):
                sp.wait_ge(out_stored[g], 16 * GRAPHS // GROUP)

        @block.gpsimd
        def _(pool):
            pool.memset(ident[:, :], 0.0).then_inc(ident_zero, 1)
            pool.memset(half_neg[:, :], -0.5).then_inc(ident_zero, 1)
            pool.memset(eps_col[:, :], EPS).then_inc(ident_zero, 1)
            pool.wait_ge(ident_zero, 3)
            pool.affine_select(out=ident[:, :], in_=ident[:, :], compare_op=ALU.not_equal, fill=1.0,
                               base=0, pattern=[[-1, P]], channel_multiplier=1).then_inc(ident_done, 1)

            def inv_std(slot, n, lag, count=1):
                add_eps(slot, n, lag, count)
                power(slot, n, lag, count)

            def add_eps(slot, n, lag, count=1):
                slot.wait(pool, mv_done[n], lag)
                var = mv[n][:, slot.buf(lag, 2) if count == 1 else 0, :].rearrange("p (g t) -> p g t", t=2)[:, :, 1]
                pool.tensor_tensor(ve[n][:, :], var, eps_col[:, 0:1].to_broadcast([P, count]), ALU.add)\
                    .then_inc(ve_done[n], count)

            def power(slot, n, lag, count=1):
                slot.wait(pool, ve_done[n], lag)
                pool.tensor_tensor(rs[n][:, slot.buf(lag, 2) if count == 1 else 0, :], ve[n][:, :],
                                   half_neg[:, 0:1].to_broadcast([P, count]), ALU.pow)\
                    .then_inc(rs_done[n], count)

            def emit(slot):
                if slot.on(L_V):
                    slot.wait(pool, x3_done, L_V)
                    slot.wait(pool, out_done, L_V, BUFS)
                    pool.tensor_tensor(x4[:, slot.buf(L_V, BUFS), :], x3[:, slot.buf(L_V, 2), :],
                                       bv_row[:, :], ALU.add).then_inc(x4_init, 1)
                if slot.on(L_GCN):
                    slot.wait(pool, x2_done, L_GCN)
                    slot.wait(pool, r2_done, L_GCN, 1)
                    pool.tensor_tensor(x2b[:, :], x2[:, slot.buf(L_GCN, 2), :], bias2[:, :], ALU.add)\
                        .then_inc(x2b_done, 1)
                if slot.on(L_EDGE):
                    slot.wait(pool, x_hi_done, L_EDGE)
                    slot.wait(pool, edge_mm, L_EDGE, 1)
                    pool.tensor_tensor(x_lo[:, :], x_in[:, slot.buf(L_EDGE, 4), :], x_hi[:, :].bitcast(F32),
                                       ALU.subtract).then_inc(x_lo_done, 1)
                if slot.on(L_GAT):
                    slot.wait(pool, e1_done, L_GAT)
                if slot.on(L_EDGE):
                    add_eps(slot, "0", L_EDGE)
                if slot.on(L_GAT):
                    b2 = slot.buf(L_GAT, 2)
                    pool.tensor_scalar(e1[:, :], e1[:, :], 1.0, -1.0, ALU.min, ALU.add)\
                        .then_inc(e1m_done, 1)
                if slot.on(L_EDGE):
                    power(slot, "0", L_EDGE)
                if slot.on(L_GAT):
                    slot.wait(pool, e1m_done, L_GAT)
                    slot.wait(pool, r1_done, L_GAT)
                    pool.tensor_tensor(r1[:, b2, :], r1[:, b2, :], e1[:, :], ALU.add)\
                        .then_inc(r1_sum_done, 1)
                if slot.on(L_PV):
                    k, first = slot.part(L_PV), slot.buf(L_PV, BUFS) // GROUP * GROUP
                    slot.wait(pool, o_norm_done, L_PV)
                    if k == 0:
                        slot.wait(pool, x4_init, L_PV - (GROUP - 1))
                    res = x4[:, first:first + GROUP, k * CHUNKS * P:(k + 1) * CHUNKS * P]
                    pool.tensor_tensor(res, res, o_norm[:, :, :], ALU.add).then_inc(x4_done, 1)
                if slot.on(L_GAT):
                    inv_std(slot, "1", L_GAT)
                if slot.on(L_GCN):
                    inv_std(slot, "2", L_GCN)
                if slot.on(L_PV) and slot.part(L_PV) == GROUP - 1:
                    inv_std(slot, "3", L_PV, GROUP)
            slots(pool, emit)

        @block.scalar
        def _(act):
            def split_weight(n):
                act.wait_ge(w_in[n % 2], 16 * (n // 2 + 1))
                act.activation(weights[w_order[n]][0][:, :, :], stage[n % 2], ACT.Copy).then_inc(w_hi_done, 1)

            act.wait_ge(setup_mm, 1)
            act.activation(adj_t_hi[:, :], att_bank[:, 0:P], ACT.Copy).then_inc(adj_hi_done, 1)
            split_weight(0)

            def project(dst, bank, bias, mm, done, slot):
                slot.wait(act, mm, L_QK)
                slot.wait(act, score_mm, L_QK, 1)
                for c in range(CHUNKS):
                    chunk = slot.part(L_QK) * CHUNKS + c
                    ins = act.activation(dst[:, c, :], bank[:, c * GROUP * P:(c + 1) * GROUP * P],
                                         ACT.Identity, bias=bias[:, chunk:chunk + 1])
                ins.then_inc(done, 1)

            def emit(slot):
                for n in range(1, len(w_order)):
                    if slot.first(n):
                        split_weight(n)
                if Slot(slot.base, slot.offset - 1).on(L_V):
                    lag = L_V + 1
                    slot.wait(act, v_mm, lag)
                    slot.wait(act, pv_mm, L_PV, 1)
                    act.activation(v_sb[:, slot.buf(lag, BUFS), :], rot[3][:, :], ACT.Copy)\
                        .then_inc(v_done, 1)
                if slot.on(L_QK):
                    project(q_sb, rot[0], qb_col, q_mm, q_done, slot)
                if slot.on(L_GAT):
                    slot.wait(act, z1_mm, L_GAT, 1)
                    slot.wait(act, y1_mm, L_GAT)
                    act.activation(y1_hi[:, :], rot[1][:, :], ACT.Copy).then_inc(y1_hi_done, 1)
                if slot.on(L_EDGE):
                    b4 = slot.buf(L_EDGE, 4)
                    act.wait_ge(x_loaded[b4], (slot.graph(L_EDGE) - b4) * 4 + 16)
                    slot.wait(act, edge_mm, L_EDGE, 1)
                    slot.wait(act, x_lo_done, L_EDGE, 1)
                    act.activation(x_hi[:, :], x_in[:, b4, :], ACT.Copy).then_inc(x_hi_done, 1)
                if slot.on(L_ATT):
                    b2, b4 = slot.buf(L_ATT, 2), slot.buf(L_ATT, 4)
                    slot.wait(act, s2_mm, L_ATT)
                    slot.wait(act, lrelu_done, L_ATT, 2)
                    act.activation(z0[:, b2, :], s2_bank[:, 0:P], ACT.Identity,
                                   bias=s1_col[:, b4:b4 + 1]).then_inc(z0_done, 1)
                if slot.on(L_ATT):
                    slot.wait(act, att_nmax_done, L_ATT)
                    slot.wait(act, att_n_done, L_ATT, 2)
                    act.activation(att_p[:, b2, :], att_e[:, b2, :], ACT.Exp, bias=att_nmax[:, b2:b2 + 1],
                                   accum_out=att_sum[:, b2:b2 + 1]).then_inc(att_exp, 1)
                if slot.on(L_QK):
                    project(k_sb, rot[2], kb_col, k_mm, k_done, slot)
                if slot.on(L_PV):
                    slot.wait(act, pt0_mm, L_PV)
                    slot.wait(act, pv_mm, L_PV, 1)
                    act.activation(probs_t[:, 0, :, :].rearrange("p t n -> p (t n)"), rot[3][:, :], ACT.Copy)\
                        .then_inc(pt0_done, 1)
                    slot.wait(act, pt1_mm, L_PV)
                    act.activation(probs_t[:, 1, :, :].rearrange("p t n -> p (t n)"), rot[0][:, :], ACT.Copy)\
                        .then_inc(pt1_done, 1)
                if slot.on(L_GAT):
                    slot.wait(act, z1_mm, L_GAT)
                    slot.wait(act, r1_sum_done, L_GAT, 1)
                    act.activation(e1[:, :], rot[1][:, :], ACT.Exp).then_inc(e1_done, 1)
                if slot.on(L_GCN):
                    slot.wait(act, z2_mm, L_GCN, 1)
                    slot.wait(act, y2_mm, L_GCN)
                    act.activation(y2_hi[:, :], rot[2][:, :], ACT.Copy).then_inc(y2_hi_done, 1)
                if slot.on(L_ATT):
                    slot.wait(act, att_t_mm, L_ATT)
                    slot.wait(act, y1_mm, L_ATT, 2)
                    act.activation(att_t[:, b2, :], att_bank[:, 0:P], ACT.Copy).then_inc(att_t_done, 1)
                if slot.on(L_TR):
                    buf = slot.buf(L_TR, BUFS)
                    slot.wait(act, xt_mm, L_TR)
                    slot.wait(act, k_mm, L_QK)
                    slot.wait(act, v_mm, L_TR, BUFS)
                    act.activation(xt_hi[:, :, buf, :], rot[2][:, :].rearrange("p (k n) -> p k n", k=KC),
                                   ACT.Copy).then_inc(xt_hi_done, 1)
                if slot.on(L_QK):
                    par = slot.buf(L_QK, 2)
                    slot.wait(act, score_nmax_done, L_QK)
                    slot.wait(act, pt1_mm, L_QK, 2)
                    slot.wait(act, inv_done, L_QK, 2)
                    for h in range(2):
                        for t in range(TILES):
                            c, g = divmod(t, GROUP)
                            i = (g * CHUNKS + c) * 2 + h
                            ins = act.activation(probs[:, par, h, t, :], s_masked[:, h, t, :], ACT.Exp,
                                                 bias=sc_nmax[:, h, t:t + 1], scale=SCALE,
                                                 accum_out=sc_sum[:, par, i:i + 1])
                    ins.then_inc(score_exp, 1)

            slots(act, emit)

        @block.vector
        def _(dve):
            dve.wait_ge(ident_done, 1)
            dve.wait_ge(const_in, 16 * 8)
            dve.tensor_scalar(mask[:, :], adj_sb[:, :], 0.0, MASKED, ALU.is_equal, ALU.mult)\
               .then_inc(consts_done, 1)
            dve.tensor_scalar(beta_i[:, :], ident[:, :], beta_col[:, 0:1], None, ALU.mult)\
               .then_inc(consts_done, 1)
            dve.wait_ge(setup_mm, 1)
            dve.wait_ge(adj_hi_done, 1)
            dve.tensor_copy(adj_t[:, :], att_bank[:, 0:P])
            dve.tensor_tensor(adj_t_lo[:, :], att_bank[:, 0:P], adj_t_hi[:, :].bitcast(F32), ALU.subtract)\
               .then_inc(setup_copied, 1)
            dve.wait_ge(setup_mm, 2)
            for c in range(KC):
                ins = dve.tensor_copy(w_t[:, c, :], rot[c][:, :])
            ins.then_inc(setup_copied, 1)
            dve.wait_ge(setup_mm, 3)
            dve.tensor_copy(u1[:, :], score_bank[0][:, :])
            dve.tensor_copy(u2[:, :], score_bank[1][:, :]).then_inc(setup_copied, 1)

            def split_weight(n):
                dve.wait_ge(w_hi_done, n + 1)
                dve.tensor_tensor(weights[w_order[n]][1][:, :, :], stage[n % 2],
                                  weights[w_order[n]][0][:, :, :].bitcast(F32), ALU.subtract)\
                   .then_inc(w_lo_done, 1)

            split_weight(0)

            def statistics(n, src, g=0):
                dve.bn_stats(st[n][:, 6 * g:6 * g + 6], src).then_inc(st_done[n], 1)

            def aggregate(n, par, count=1):
                for g in range(count):
                    dve.bn_aggr(mv[n][:, par, 2 * g:2 * g + 2], st[n][:, 6 * g:6 * g + 6])\
                       .then_inc(mv_done[n], 1)

            def emit(slot):
                for n in range(1, len(w_order)):
                    if slot.first(n):
                        split_weight(n)
                if slot.on(L_GAT):
                    slot.wait(dve, y1_hi_done, L_GAT)
                    dve.tensor_tensor(y1_lo[:, :], rot[1][:, :], y1_hi[:, :].bitcast(F32), ALU.subtract)\
                        .then_inc(y1_lo_done, 1)
                if slot.on(L_ATT):
                    a2 = slot.buf(L_ATT, 2)
                    slot.wait(dve, z0_done, L_ATT)
                    slot.wait(dve, att_max_done, L_ATT, 2)
                    dve.scalar_tensor_tensor(out=lrelu[:, a2, :], in0=z0[:, a2, :], scalar=SLOPE,
                                             in1=z0[:, a2, :], op0=ALU.mult, op1=ALU.max)\
                        .then_inc(lrelu_done, 1)
                    slot.wait(dve, lrelu_done, L_ATT)
                    slot.wait(dve, att_exp, L_ATT, 2)
                if slot.on(L_EDGE):
                    b4 = slot.buf(L_EDGE, 4)
                    dve.wait_ge(x_loaded[b4], (slot.graph(L_EDGE) - b4) * 4 + 16)
                    statistics("0", x_in[:, b4, :])
                if slot.on(L_ATT):
                    dve.tensor_tensor_reduce(out=att_e[:, a2, :], in0=lrelu[:, a2, :], in1=adj_sb[:, :],
                                             scale=1.0, scalar=-3.0e38, op0=ALU.mult, op1=ALU.max,
                                             accum_out=att_max[:, a2:a2 + 1]).then_inc(att_max_done, 1)
                if slot.on(L_EDGE):
                    slot.wait(dve, st_done["0"], L_EDGE)
                if slot.on(L_ATT):
                    slot.wait(dve, att_max_done, L_ATT)
                    dve.tensor_scalar(att_nmax[:, a2:a2 + 1], att_max[:, a2:a2 + 1], -1.0, None, ALU.mult)\
                        .then_inc(att_nmax_done, 1)
                if slot.on(L_EDGE):
                    aggregate("0", slot.buf(L_EDGE, 2))
                if slot.on(L_ATT):
                    slot.wait(dve, att_exp, L_ATT)
                    dve.reciprocal(att_inv[:, a2:a2 + 1], att_sum[:, a2:a2 + 1]).then_inc(att_inv_done, 1)
                    slot.wait(dve, att_inv_done, L_ATT)
                    slot.wait(dve, att_t_mm, L_ATT, 2)
                    dve.scalar_tensor_tensor(out=att_n[:, a2, :], in0=att_p[:, a2, :],
                                             scalar=att_inv[:, a2:a2 + 1], in1=beta_i[:, :],
                                             op0=ALU.mult, op1=ALU.add).then_inc(att_n_done, 1)
                if slot.on(L_PV):
                    par = slot.buf(L_PV, 2)
                    slot.wait(dve, score_exp, L_PV)
                    slot.wait(dve, o_norm_done, L_PV, 1)
                    dve.reciprocal(sc_inv[:, :], sc_sum[:, par, :]).then_inc(inv_done, 1)
                if slot.on(L_GAT):
                    g2, g4 = slot.buf(L_GAT, 2), slot.buf(L_GAT, 4)
                    slot.wait(dve, e1_done, L_GAT)
                    slot.wait(dve, x2_done, L_GAT, 2)
                    dve.scalar_tensor_tensor(out=r1[:, g2, :], in0=rot[1][:, :], scalar=0.0,
                                             in1=x1[:, g4, :], op0=ALU.max, op1=ALU.add)\
                        .then_inc(r1_done, 1)
                if slot.on(L_GCN):
                    slot.wait(dve, y2_hi_done, L_GCN)
                    dve.tensor_tensor(y2_lo[:, :], rot[2][:, :], y2_hi[:, :].bitcast(F32), ALU.subtract)\
                        .then_inc(y2_lo_done, 1)
                if slot.on(L_PV):
                    slot.wait(dve, pv_mm, L_PV)
                    slot.wait(dve, inv_done, L_PV)
                    slot.wait(dve, x4_done, L_PV, 1)
                    dve.tensor_tensor(o_norm[:, :, :].rearrange("p g (c d) -> p (g c) d", d=HEAD),
                                      rot[3][:, :].rearrange("p (h d) -> p h d", d=HEAD),
                                      sc_inv[:, :].unsqueeze(2).to_broadcast([P, 2 * TILES, HEAD]),
                                      ALU.mult).then_inc(o_norm_done, 1)
                if slot.on(L_EDGE):
                    slot.wait(dve, edge_mm, L_EDGE)
                    dve.tensor_reduce(edge_max[:, :], rot[0][:, :], axis=AX.X, op=ALU.max)\
                        .then_inc(edge_max_done, 1)
                    slot.wait(dve, edge_max_done, L_EDGE)
                    dve.tensor_scalar(edge_c[:, :], edge_max[:, :], b0_col[:, 0:1], 0.0, ALU.add, ALU.max)\
                        .then_inc(edge_c_done, 1)
                if slot.on(L_EDGE):
                    e2 = slot.buf(L_EDGE, 2)
                    slot.wait(dve, edge_c_done, L_EDGE)
                    slot.wait(dve, mv_done["0"], L_EDGE)
                    dve.tensor_tensor(edge_m[:, :], mv["0"][:, e2, 0:1], edge_c[:, :], ALU.add)\
                        .then_inc(edge_m_done, 1)
                    slot.wait(dve, edge_m_done, L_EDGE)
                    dve.tensor_tensor(edge_d[:, :], edge_c[:, :], edge_m[:, :], ALU.subtract)\
                        .then_inc(edge_d_done, 1)
                    slot.wait(dve, edge_d_done, L_EDGE)
                    slot.wait(dve, rs_done["0"], L_EDGE)
                    slot.wait(dve, y1_mm, L_EDGE, 4)
                    dve.tensor_scalar(x1[:, b4, :], x_in[:, b4, :], edge_d[:, 0:1], rs["0"][:, e2, 0:1],
                                      ALU.add, ALU.mult).then_inc(x1_done, 1)
                if slot.on(L_TR):
                    buf = slot.buf(L_TR, BUFS)
                    slot.wait(dve, xt_hi_done, L_TR)
                    dve.tensor_tensor(xt_lo[:, :, buf, :], rot[2][:, :].rearrange("p (k n) -> p k n", k=KC),
                                      xt_hi[:, :, buf, :].bitcast(F32), ALU.subtract).then_inc(xt_lo_done, 1)
                if slot.on(L_EDGE):
                    slot.wait(dve, x1_done, L_EDGE)
                    for n, (u, s) in enumerate(((u1, s1_col), (u2, s2_col))):
                        ins = dve.tensor_tensor_reduce(out=dot_tmp[:, n, :], in0=x1[:, b4, :], in1=u[:, :],
                                                       scale=1.0, scalar=0.0, op0=ALU.mult, op1=ALU.add,
                                                       accum_out=s[:, b4:b4 + 1])
                    ins.then_inc(dots_done, 1)
                if slot.on(L_GAT):
                    slot.wait(dve, r1_sum_done, L_GAT)
                    statistics("1", r1[:, g2, :])
                    slot.wait(dve, st_done["1"], L_GAT)
                for h in range(2):
                    if slot.on(L_QK):
                        slot.wait(dve, score_mm, L_QK)
                        slot.wait(dve, score_exp, L_QK, 1)
                        dve.tensor_tensor(s_masked[:, h, :, :], score_bank[h][:, :].rearrange("p (t n) -> p t n", n=P),
                                          mask[:, :].unsqueeze(1).to_broadcast([P, TILES, P]), ALU.add)\
                            .then_inc(masked_done, 1)
                    if slot.on(L_GAT) and h == 0:
                        aggregate("1", g2)
                if slot.on(L_QK):
                    dve.wait_ge(masked_done, slot.graph(L_QK) * 2 + 2)
                    dve.tensor_reduce(sc_max[:, :, :].rearrange("p h t -> p (h t)"),
                                      s_masked[:, :, :, :].rearrange("p h t n -> p (h t) n"),
                                      axis=AX.X, op=ALU.max).then_inc(score_max_done, 1)
                    slot.wait(dve, score_max_done, L_QK)
                    dve.tensor_scalar(sc_nmax[:, :, :], sc_max[:, :, :], -SCALE, None, ALU.mult)\
                        .then_inc(score_nmax_done, 1)
                last = slot.on(L_PV) and slot.part(L_PV) == GROUP - 1
                if last:
                    first = slot.buf(L_PV, BUFS) // GROUP * GROUP
                    slot.wait(dve, x4_done, L_PV)
                    for g in range(GROUP):
                        statistics("3", x4[:, first + g, :], g)
                    slot.wait(dve, st_done["3"], L_PV)
                if slot.on(L_GCN):
                    slot.wait(dve, z2_mm, L_GCN)
                    slot.wait(dve, x2b_done, L_GCN)
                    slot.wait(dve, x3_done, L_GCN, 1)
                    dve.tensor_tensor(r2[:, :], rot[1][:, :], x2b[:, :], ALU.add).then_inc(r2_done, 1)
                if last:
                    aggregate("3", 0, GROUP)
                if slot.on(L_GCN):
                    slot.wait(dve, r2_done, L_GCN)
                    statistics("2", r2[:, :])
                    slot.wait(dve, st_done["2"], L_GCN)
                if slot.on(L_GAT):
                    slot.wait(dve, rs_done["1"], L_GAT)
                    slot.wait(dve, x2b_done, L_GAT, 2)
                    slot.wait(dve, y2_mm, L_GAT, 2)
                    dve.tensor_scalar(x2[:, g2, :], r1[:, g2, :], mv["1"][:, g2, 0:1], rs["1"][:, g2, 0:1],
                                      ALU.subtract, ALU.mult).then_inc(x2_done, 1)
                if slot.on(L_GCN):
                    aggregate("2", slot.buf(L_GCN, 2))
                    c2 = slot.buf(L_GCN, 2)
                    slot.wait(dve, rs_done["2"], L_GCN)
                    slot.wait(dve, xt_mm, L_GCN, 2)
                    slot.wait(dve, x4_init, L_GCN, 2)
                    dve.tensor_scalar(x3[:, c2, :], r2[:, :], mv["2"][:, c2, 0:1], rs["2"][:, c2, 0:1],
                                      ALU.subtract, ALU.mult).then_inc(x3_done, 1)
                if slot.on(L_PV) and slot.part(L_PV) == GROUP - 1:
                    slot.wait(dve, rs_done["3"], L_PV)
                    for g in range(GROUP):
                        stored = (slot.graph(L_PV) - (GROUP - 1)) * (16 // GROUP)
                        if not (isinstance(stored, int) and stored <= 0):
                            dve.wait_ge(out_stored[g], stored)
                        ins = dve.tensor_scalar(out_sb[:, g, :], x4[:, first + g, :],
                                                mv["3"][:, 0, 2 * g:2 * g + 1], rs["3"][:, 0, g:g + 1],
                                                ALU.subtract, ALU.mult)
                        ins.then_inc(out_done, 1)

            slots(dve, emit)

        @block.tensor
        def _(pe):
            def three(outp, lhs, rhs, first, last):
                (lh, ll), (rh, rl) = lhs, rhs
                pe.matmul(outp, lh, rh, start=first, stop=False)
                pe.matmul(outp, lh, rl, start=False, stop=False)
                return pe.matmul(outp, ll, rh, start=False, stop=last)

            def dense(bank, lhs, w):
                for k in range(KC):
                    ins = three(bank[:, :], [a[:, k, :] for a in lhs], [b[:, k, :] for b in weights[w]],
                                k == 0, k == KC - 1)
                return ins

            pe.wait_ge(ident_done, 1)
            pe.wait_ge(const_in, 16 * 8)
            pe.transpose(att_bank[:, 0:P], adj_sb[:, :], ident[:, :]).then_inc(setup_mm, 1)
            pe.wait_ge(w_in[0], 16)
            for f in range(KC):
                for c in range(KC):
                    ins = pe.transpose(rot[f][:, c * P:(c + 1) * P], stage[0][:, c, f * P:(f + 1) * P], ident[:, :])
            ins.then_inc(setup_mm, 1)
            pe.wait_ge(setup_copied, 2)
            for n in range(2):
                for f in range(KC):
                    ins = pe.matmul(score_bank[n][:, :], a_col[:, n * KC + f:n * KC + f + 1].to_broadcast([P, P]),
                                    w_t[:, f, :], start=f == 0, stop=f == KC - 1)
            ins.then_inc(setup_mm, 1)
            pe.wait_ge(setup_copied, 3)

            def weight_split(slot, w, lag):
                if slot.first(lag):
                    pe.wait_ge(w_lo_done, w_order.index(w) + 1)

            y1 = [a[:, :].rearrange("p (k n) -> p k n", k=KC) for a in (y1_hi, y1_lo)]
            y2 = [a[:, :].rearrange("p (k n) -> p k n", k=KC) for a in (y2_hi, y2_lo)]

            def projection(bank, w, slot):
                first = slot.buf(L_QK, BUFS) // GROUP * GROUP
                for c in range(CHUNKS):
                    chunk = slot.part(L_QK) * CHUNKS + c
                    for k in range(KC):
                        ins = three(bank[:, c * GROUP * P:(c + 1) * GROUP * P],
                                    [a[:, k, chunk * P:(chunk + 1) * P] for a in weights[w]],
                                    [b[:, k, first:first + GROUP, :].rearrange("p g n -> p (g n)") for b in (xt_hi, xt_lo)],
                                    k == 0, k == KC - 1)
                return ins

            def emit(slot):
                if slot.on(L_QK):
                    weight_split(slot, "wk", L_QK)
                    if slot.part(L_QK) == 0:
                        slot.wait(pe, xt_lo_done, L_QK - (GROUP - 1))
                    slot.wait_last(pe, (edge_max_done, L_EDGE, 1), (pt1_done, L_PV, 1))
                    projection(rot[0], "wq", slot).then_inc(q_mm, 1)
                if slot.on(L_ATT):
                    b4 = slot.buf(L_ATT, 4)
                    slot.wait(pe, dots_done, L_ATT)
                    slot.wait(pe, z0_done, L_ATT, 1)
                    pe.transpose(s2_bank[:, 0:P], s2_col[:, b4:b4 + 1].to_broadcast([P, P]), ident[:, :])\
                      .then_inc(s2_mm, 1)
                if slot.on(L_GAT):
                    g2, g4 = slot.buf(L_GAT, 2), slot.buf(L_GAT, 4)
                    slot.wait(pe, att_t_done, L_GAT)
                    slot.wait_last(pe, (r2_done, L_GCN, 1), (r1_done, L_GAT, 1))
                    slot.wait(pe, r1_done, L_GAT, 1)
                    for k in range(KC):
                        ins = pe.matmul(rot[1][:, k * P:(k + 1) * P], x1[:, g4, k * P:(k + 1) * P],
                                        att_t[:, g2, :], start=True, stop=True)
                    ins.then_inc(y1_mm, 1)
                if slot.on(L_QK):
                    slot.wait_last(pe, (xt_lo_done, L_TR, 1), (y2_lo_done, L_GCN, 1), (k_done, L_QK, 1))
                    projection(rot[2], "wk", slot).then_inc(k_mm, 1)
                if slot.on(L_PV):
                    par = slot.buf(L_PV, 2)
                    slot.wait(pe, score_exp, L_PV)
                    slot.wait_last(pe, (v_done, L_V, 1), (o_norm_done, L_PV, 1))
                    for t in range(TILES):
                        ins = pe.transpose(rot[3][:, t * P:(t + 1) * P], probs[:, par, 0, t, :], ident[:, :])
                    ins.then_inc(pt0_mm, 1)
                    slot.wait_last(pe, (q_done, L_QK, 0), (pt1_done, L_PV, 1))
                    for t in range(TILES):
                        ins = pe.transpose(rot[0][:, t * P:(t + 1) * P], probs[:, par, 1, t, :], ident[:, :])
                    ins.then_inc(pt1_mm, 1)
                if slot.on(L_GAT):
                    slot.wait(pe, y1_lo_done, L_GAT)
                    weight_split(slot, "w1", L_GAT)
                    dense(rot[1], y1, "w1").then_inc(z1_mm, 1)
                if slot.on(L_GCN):
                    slot.wait(pe, x2_done, L_GCN)
                    slot.wait_last(pe, (k_done, L_QK, 0), (xt_lo_done, L_TR, 1), (y2_lo_done, L_GCN, 1))
                    for k in range(KC):
                        ins = pe.matmul(rot[2][:, k * P:(k + 1) * P], x2[:, slot.buf(L_GCN, 2), k * P:(k + 1) * P],
                                        adj_t[:, :], start=True, stop=True)
                    ins.then_inc(y2_mm, 1)
                if slot.on(L_PV):
                    slot.wait(pe, pt0_done, L_PV)
                    slot.wait(pe, pt1_done, L_PV)
                    if slot.part(L_PV) == 0:
                        slot.wait(pe, v_done, L_PV - (GROUP - 1))
                    first = slot.buf(L_PV, BUFS) // GROUP * GROUP
                    for g in range(GROUP):
                        for c in range(CHUNKS):
                            for h in range(2):
                                at = ((g * CHUNKS + c) * 2 + h) * HEAD
                                col = (slot.part(L_PV) * CHUNKS + c) * P + h * HEAD
                                ins = pe.matmul(rot[3][:, at:at + HEAD], probs_t[:, h, c * GROUP + g, :],
                                                v_sb[:, first + g, col:col + HEAD], start=True, stop=True)
                    ins.then_inc(pv_mm, 1)
                if slot.on(L_ATT):
                    slot.wait(pe, att_n_done, L_ATT)
                    slot.wait(pe, att_t_done, L_ATT, 1)
                    pe.transpose(att_bank[:, 0:P], att_n[:, slot.buf(L_ATT, 2), :], ident[:, :])\
                      .then_inc(att_t_mm, 1)
                if slot.on(L_EDGE):
                    b4 = slot.buf(L_EDGE, 4)
                    slot.wait(pe, x_lo_done, L_EDGE)
                    slot.wait_last(pe, (pt1_done, L_PV, 0), (q_done, L_QK, 0), (edge_max_done, L_EDGE, 1))
                    three(rot[0][:, :], (adj_t_hi[:, :], adj_t_lo[:, :]), (x_hi[:, :], x_lo[:, :]), True, True)\
                        .then_inc(edge_mm, 1)
                if slot.on(L_TR):
                    slot.wait(pe, x3_done, L_TR)
                    slot.wait_last(pe, (y2_lo_done, L_GCN, 0), (k_done, L_QK, 0), (xt_lo_done, L_TR, 1))
                    for k in range(KC):
                        ins = pe.transpose(rot[2][:, k * P:(k + 1) * P], x3[:, slot.buf(L_TR, 2), k * P:(k + 1) * P],
                                           ident[:, :])
                    ins.then_inc(xt_mm, 1)
                if slot.on(L_QK):
                    slot.wait(pe, q_done, L_QK)
                    slot.wait(pe, k_done, L_QK)
                    masked = slot.graph(L_QK) * 2
                    if not (isinstance(masked, int) and masked == 0):
                        pe.wait_ge(masked_done, masked)
                    for t in range(TILES):
                        c, g = divmod(t, GROUP)
                        for h in range(2):
                            rows, cols = slice(h * HEAD, (h + 1) * HEAD), slice(g * P, (g + 1) * P)
                            ins = pe.matmul(score_bank[h][:, t * P:(t + 1) * P], q_sb[rows, c, cols],
                                            k_sb[rows, c, cols], start=True, stop=True)
                    ins.then_inc(score_mm, 1)
                if slot.on(L_GCN):
                    slot.wait(pe, y2_lo_done, L_GCN)
                    weight_split(slot, "w2", L_GCN)
                    slot.wait_last(pe, (r1_done, L_GAT, 0), (r2_done, L_GCN, 1))
                    dense(rot[1], y2, "w2").then_inc(z2_mm, 1)
                if slot.on(L_V):
                    buf = slot.buf(L_V, BUFS)
                    slot.wait(pe, xt_lo_done, L_V)
                    weight_split(slot, "wv", L_V)
                    slot.wait_last(pe, (o_norm_done, L_PV, 0), (v_done, L_V, 1))
                    dense(rot[3], [a[:, :, buf, :] for a in (xt_hi, xt_lo)], "wv").then_inc(v_mm, 1)

            slots(pe, emit)


_INS = ["x", "adj", "L0_gnn_b", "L1_gnn_W", "L1_gnn_a", "L1_gnn_beta", "L2_gnn_weight", "L2_gnn_bias",
        "L3_gnn_Wq", "L3_gnn_bq", "L3_gnn_Wk", "L3_gnn_bk", "L3_gnn_Wv", "L3_gnn_bv"]


def kernel(**inputs):
    import numpy as _np
    import concourse.bacc as _bacc
    from concourse import mybir as _mybir
    from concourse.bass_utils import run_bass_kernel_spmd as _run

    nc = _bacc.Bacc("TRN2", target_bir_lowering=False, num_devices=1)
    arrays, args = {}, []
    for name in _INS:
        a = _np.ascontiguousarray(inputs[name])
        arrays[f"in_{name}"] = a
        args.append(nc.dram_tensor(f"in_{name}", a.shape, _mybir.dt.from_np(a.dtype), kind="ExternalInput").ap())
    args.append(nc.dram_tensor("out_x", (GRAPHS, NODES, FEATS), _mybir.dt.float32, kind="ExternalOutput").ap())
    graph_layers_kernel(nc, *args)
    r = _run(nc, [arrays], core_ids=[0])
    return r.results[0]["out_x"]
```

```python
from contextlib import ExitStack

import concourse.bass as bass
from concourse import mybir

F32 = mybir.dt.float32
F32R = mybir.dt.float32r
ALU = mybir.AluOpType
ACT = mybir.ActivationFunctionType
AX = mybir.AxisListType

GRAPHS, NODES, FEATS = 128, 128, 512
P = 128
KC = FEATS // P
HEAD = 64
GROUP = 2
BUFS = 2 * GROUP
CHUNKS = KC // GROUP
TILES = 2 * GROUP
EPS = 1e-5
SLOPE = 0.2
SCALE = 1.0 / 8.0
MASKED = -1.0e9 / SCALE

HEAD_ROWS = (slice(0, HEAD), slice(HEAD, P))

L_LOAD = -3
L_EDGE = 0
L_ATT = 1
L_GAT = 2
L_GCN = 3
L_TR = 4
L_V = 5
L_QK = GROUP + 4
L_PV = L_QK + 1
L_OUT = L_PV + 1
WARM = -(-(L_OUT + 2) // BUFS) * BUFS
LOOP_END = WARM + (GRAPHS + L_LOAD - WARM) // BUFS * BUFS
SLOTS = GRAPHS + L_OUT


class Slot:

    def __init__(self, base, offset):
        self.base, self.offset = base, offset

    def on(self, lag):
        return not isinstance(self.base, int) or 0 <= self.base + self.offset - lag < GRAPHS

    def first(self, lag):
        return isinstance(self.base, int) and self.base + self.offset == lag

    def graph(self, lag):
        return self.base + (self.offset - lag)

    def buf(self, lag, count):
        return (self.offset - lag) % count

    def part(self, lag):
        return (self.offset - lag) % GROUP

    def wait(self, eng, sem, lag, ago=0):
        value = self.base + (self.offset - lag - ago + 1)
        if not isinstance(self.base, int):
            eng.wait_ge(sem, value)
        elif min(value, GRAPHS) > 0:
            eng.wait_ge(sem, min(value, GRAPHS))

    def wait_last(self, eng, *jobs):
        for sem, lag, ago in jobs:
            if Slot(self.base, self.offset - ago).on(lag):
                Slot(self.base, self.offset - ago).wait(eng, sem, lag)
                return


def slots(eng, emit):
    for s in range(WARM):
        emit(Slot(s - s % BUFS, s % BUFS))
    with eng.Fori(0, (LOOP_END - WARM) // BUFS) as turn:
        for c in range(BUFS):
            emit(Slot(turn * BUFS + WARM, c))
    for s in range(LOOP_END, SLOTS):
        emit(Slot(s - s % BUFS, s % BUFS))


def graph_layers_kernel(nc, x, adj, l0_b, l1_w, l1_a, l1_beta, l2_w, l2_bias,
                        wq, bq, wk, bk, wv, bv, out):
    ctx = ExitStack()
    with ctx:
        def sb(name, shape, dt=F32):
            return ctx.enter_context(nc.sbuf_tensor(name, shape, dt))

        def sem(name):
            return ctx.enter_context(nc.semaphore(name))

        weights = {n: (sb(f"{n}_hi", [P, KC, FEATS], F32R), sb(f"{n}_lo", [P, KC, FEATS], F32R))
                   for n in ("w1", "w2", "wq", "wk", "wv")}
        adj_sb = sb("adj_sb", [P, P])
        adj_t = sb("adj_t", [P, P])
        adj_t_hi, adj_t_lo = sb("adj_t_hi", [P, P], F32R), sb("adj_t_lo", [P, P], F32R)
        ident = sb("ident", [P, P])
        beta_i = sb("beta_i", [P, P])
        mask = sb("mask", [P, P])
        b0_col = sb("b0_col", [P, 1])
        beta_col = sb("beta_col", [P, 1])
        wa_col = sb("wa_col", [P, 2 * KC])
        qb_col = sb("qb_col", [P, KC])
        kb_col = sb("kb_col", [P, KC])
        half_neg = sb("half_neg", [P, 1])
        neg_one = sb("neg_one", [P, 1])
        eps_col = sb("eps_col", [P, 1])
        u1 = sb("u1", [P, FEATS])
        u2 = sb("u2", [P, FEATS])
        bias2 = sb("bias2", [P, FEATS])
        bv_row = sb("bv_row", [P, FEATS])

        x_in = sb("x_in", [P, 4, FEATS])
        x_hi, x_lo = sb("x_hi", [P, FEATS], F32R), sb("x_lo", [P, FEATS], F32R)
        x1 = sb("x1", [P, 4, FEATS])
        x2 = sb("x2", [P, 2, FEATS])
        x2b = sb("x2b", [P, FEATS])
        x3 = sb("x3", [P, 2, FEATS])
        x4 = sb("x4", [P, BUFS, FEATS])
        e1 = sb("e1", [P, FEATS])
        r1 = sb("r1", [P, 2, FEATS])
        r2 = sb("r2", [P, FEATS])
        y1_hi, y1_lo = sb("y1_hi", [P, FEATS], F32R), sb("y1_lo", [P, FEATS], F32R)
        y2_hi, y2_lo = sb("y2_hi", [P, FEATS], F32R), sb("y2_lo", [P, FEATS], F32R)
        xt_hi = sb("xt_hi", [P, KC, BUFS, P], F32R)
        xt_lo = sb("xt_lo", [P, KC, BUFS, P], F32R)
        q_hi, q_lo = (sb(f"q_{n}", [P, CHUNKS, GROUP * P], F32R) for n in ("hi", "lo"))
        k_hi, k_lo = (sb(f"k_{n}", [P, CHUNKS, GROUP, 2, P], F32R) for n in ("hi", "lo"))
        v_sb = sb("v_sb", [P, BUFS, FEATS])
        probs = sb("probs", [P, 2, CHUNKS, TILES, P])
        probs_t = sb("probs_t", [P, CHUNKS, TILES, P])
        o_norm = sb("o_norm", [P, GROUP, CHUNKS * P])

        z0 = sb("z0", [P, 2, P])
        att_e = sb("att_e", [P, 2, P])
        att_p = sb("att_p", [P, 2, P])
        att_n = sb("att_n", [P, 2, P])
        att_t = sb("att_t", [P, 2, P])
        dot_tmp = sb("dot_tmp", [P, 2, FEATS], mybir.dt.bfloat16)
        s1_col = sb("s1_col", [P, 4])
        s2_col = sb("s2_col", [P, 4])
        att_max = sb("att_max", [P, 2])
        att_nmax = sb("att_nmax", [P, 2])
        att_sum = sb("att_sum", [P, 2])
        att_inv = sb("att_inv", [P, 2])
        edge_max = sb("edge_max", [P, 1])
        edge_c = sb("edge_c", [P, 1])
        edge_m = sb("edge_m", [P, 1])
        edge_d = sb("edge_d", [P, 1])
        st = {n: sb(f"st_{n}", [P, 6 * k]) for n, k in (("0", 1), ("1", 1), ("2", 1), ("3", GROUP))}
        mv = {n: sb(f"mv_{n}", [P, 2, 2 * k]) for n, k in (("0", 1), ("1", 1), ("2", 1), ("3", GROUP))}
        ve = {n: sb(f"ve_{n}", [P, k]) for n, k in (("0", 1), ("1", 1), ("2", 1), ("3", GROUP))}
        rs = {n: sb(f"rs_{n}", [P, 2, k]) for n, k in (("0", 1), ("1", 1), ("2", 1), ("3", GROUP))}
        out_shift = sb("out_shift", [P, GROUP])
        neg_mean = sb("neg_mean", [P, GROUP])
        sc_nmax = sb("sc_nmax", [P, CHUNKS, TILES])
        sc_sum = sb("sc_sum", [P, 2, CHUNKS * TILES])
        sc_inv = sb("sc_inv", [P, CHUNKS * TILES])

        rot = [ctx.enter_context(nc.psum_tensor(f"rot{n}", [P, 512], F32)) for n in range(4)]
        score_bank = [ctx.enter_context(nc.psum_tensor(f"score{n}", [P, 512], F32)) for n in range(2)]
        s2_bank = ctx.enter_context(nc.psum_tensor("s2_bank", [P, 512], F32))
        att_bank = ctx.enter_context(nc.psum_tensor("att_bank", [P, 512], F32))

        def q_bank(c):
            return rot[0][:, c * GROUP * P:(c + 1) * GROUP * P]

        def k_bank(c, rows):
            return rot[2][rows, c * GROUP * P:(c + 1) * GROUP * P].rearrange("p (g n) -> p g n", g=GROUP)

        stage = [probs[:, :, :, :, :].rearrange("p a b t n -> p (a b t n)").rearrange("p (k n) -> p k n", k=KC),
                 v_sb[:, :, :]]
        a_rows = x4[:, 0:2, :]
        wa_tmp = x4[:, 2:4, :]

        adj_in, a_in, const_in = sem("adj_in"), sem("a_in"), sem("const_in")
        w_in = [sem(f"w_in{n}") for n in range(2)]
        w_hi_done, w_lo_done = sem("w_hi_done"), sem("w_lo_done")
        adj_hi_done, x_hi_done, x_lo_done = sem("adj_hi_done"), sem("x_hi_done"), sem("x_lo_done")
        ident_zero, ident_done, consts_done = sem("ident_zero"), sem("ident_done"), sem("consts_done")
        u2_done = sem("u2_done")
        wa_done, k_zero = sem("wa_done"), sem("k_zero")
        setup_mm, setup_copied = sem("setup_mm"), sem("setup_copied")
        x_loaded = [sem(f"x_loaded{n}") for n in range(4)]
        out_stored = [sem(f"out_stored{n}") for n in range(GROUP)]
        (s2_mm, q_mm, y1_mm, k_mm, pt0_mm, pt1_mm, att_t_mm, z1_mm, y2_mm, pv_mm, edge_mm, score_mm,
         z2_mm, xt_mm, v_mm) = (sem(n) for n in (
            "s2_mm", "q_mm", "y1_mm", "k_mm", "pt0_mm", "pt1_mm", "att_t_mm", "z1_mm", "y2_mm",
            "pv_mm", "edge_mm", "score_mm", "z2_mm", "xt_mm", "v_mm"))
        (z0_done, q_hi_done, y1_hi_done, att_exp, k_hi_done, pt0_done, att_t_done, e1_done,
         y2_hi_done, score_exp, xt_hi_done, v_done, out_done) = (sem(n) for n in (
            "z0_done", "q_hi_done", "y1_hi_done", "att_exp", "k_hi_done", "pt0_done", "att_t_done",
            "e1_done", "y2_hi_done", "score_exp", "xt_hi_done", "v_done", "out_done"))
        (q_lo_done, lrelu_done, att_max_done, att_nmax_done, y1_lo_done, att_inv_done, att_n_done,
         pt1_done, r1_done, y2_lo_done, o_norm_done, inv_done, edge_max_done, edge_c_done,
         edge_m_done, edge_d_done, score_nmax_done, x1_done, dots_done,
         x2_done, r2_done, xt_lo_done, x3_done) = (sem(n) for n in (
            "q_lo_done", "lrelu_done", "att_max_done", "att_nmax_done", "y1_lo_done",
            "att_inv_done", "att_n_done", "pt1_done", "r1_done", "y2_lo_done",
            "o_norm_done", "inv_done", "edge_max_done", "edge_c_done", "edge_m_done", "edge_d_done",
            "score_nmax_done", "x1_done", "dots_done", "x2_done",
            "r2_done", "xt_lo_done", "x3_done"))
        st_done = {n: sem(f"st_done{n}") for n in "0123"}
        mv_done = {n: sem(f"mv_done{n}") for n in "0123"}
        ve_done = {n: sem(f"ve_done{n}") for n in "0123"}
        rs_done = {n: sem(f"rs_done{n}") for n in "0123"}
        (e1m_done, r1_sum_done, x2b_done, x4_init, x4_done) = (sem(n) for n in (
            "e1m_done", "r1_sum_done", "x2b_done", "x4_init", "x4_done"))
        k_lo_done, neg_mean_done, out_shift_done = sem("k_lo_done"), sem("neg_mean_done"), sem("out_shift_done")

        w_order = ["w1", "w2", "wv", "wq", "wk"]
        w_dram = {"w1": l1_w, "w2": l2_w, "wq": wq, "wk": wk, "wv": wv}

        block = ctx.enter_context(nc.Block())

        @block.sync
        def _(sp):
            def load(graph, buf):
                sp.dma_start(x_in[:, buf, :], x[bass.ds(graph, 1), :, :].rearrange("b i c -> i (b c)"))\
                  .then_inc(x_loaded[buf], 16)

            def load_weight(n):
                sp.dma_start(stage[n % 2], w_dram[w_order[n]].rearrange("(k p) n -> p k n", p=P))\
                  .then_inc(w_in[n % 2], 16)

            sp.dma_start(adj_sb[:, :], adj).then_inc(adj_in, 16)
            sp.dma_start(a_rows, l1_a.rearrange("(t n) o -> o t n", t=2).to_broadcast([P, 2, FEATS]),
                         allow_slow_non_contiguous=True).then_inc(a_in, 16)
            load_weight(0)
            load(0, 0)
            for dst, src in ((b0_col[:, :], l0_b.rearrange("(p o) -> p o", o=1)),
                             (beta_col[:, :], l1_beta.rearrange("(p o) -> p o", o=1).to_broadcast([P, 1])),
                             (qb_col[:, :], bq.rearrange("(k p) -> p k", p=P)),
                             (kb_col[:, :], bk.rearrange("(k p) -> p k", p=P)),
                             (bias2[:, :], l2_bias.rearrange("(o n) -> o n", o=1).to_broadcast([P, FEATS])),
                             (bv_row[:, :], bv.rearrange("(o n) -> o n", o=1).to_broadcast([P, FEATS]))):
                sp.dma_start(dst, src, allow_slow_non_contiguous=True).then_inc(const_in, 16)
            for n in range(1, -L_LOAD):
                load(n, n % 4)
                if n == 1:
                    load_weight(1)

            def emit(slot):
                if slot.on(L_LOAD):
                    buf = slot.buf(L_LOAD, 4)
                    slot.wait(sp, x_lo_done, L_LOAD, 4)
                    slot.wait(sp, x1_done, L_LOAD, 4)
                    load(slot.graph(L_LOAD), buf)
                for n in range(2, len(w_order)):
                    if slot.first(n - 1):
                        sp.wait_ge(w_lo_done, n - 1)
                        load_weight(n)
                if slot.on(L_OUT) and slot.part(L_OUT) == GROUP - 1:
                    slot.wait(sp, out_done, L_OUT)
                    first = slot.buf(L_OUT, BUFS) // GROUP * GROUP
                    for g in range(GROUP):
                        sp.dma_start(out[bass.ds(slot.graph(L_OUT + GROUP - 1 - g), 1), :, :].rearrange("b i c -> i (b c)"),
                                     x4[:, first + g, :]).then_inc(out_stored[g], 16)

            slots(sp, emit)
            for g in range(GROUP):
                sp.wait_ge(out_stored[g], 16 * GRAPHS // GROUP)

        @block.gpsimd
        def _(pool):
            pool.memset(ident[:, :], 0.0).then_inc(ident_zero, 1)
            pool.memset(half_neg[:, :], -0.5).then_inc(ident_zero, 1)
            pool.memset(eps_col[:, :], EPS).then_inc(ident_zero, 1)
            pool.memset(neg_one[:, :], -1.0).then_inc(ident_zero, 1)
            pool.wait_ge(ident_zero, 4)
            for k in (k_hi, k_lo):
                pool.memset(k[:, :, :, :, :].bitcast(F32), 0.0).then_inc(k_zero, 1)
            pool.affine_select(out=ident[:, :], in_=ident[:, :], compare_op=ALU.not_equal, fill=1.0,
                               base=0, pattern=[[-1, P]], channel_multiplier=1).then_inc(ident_done, 1)

            def split_weight(n):
                pool.wait_ge(w_hi_done, n + 1)
                pool.tensor_tensor(weights[w_order[n]][1][:, :, :], stage[n % 2],
                                  weights[w_order[n]][0][:, :, :].bitcast(F32), ALU.subtract)\
                   .then_inc(w_lo_done, 1)

            def inv_std(slot, n, lag, count=1):
                add_eps(slot, n, lag, count)
                power(slot, n, lag, count)

            def add_eps(slot, n, lag, count=1):
                slot.wait(pool, mv_done[n], lag)
                var = mv[n][:, slot.buf(lag, 2) if count == 1 else 0, :].rearrange("p (g t) -> p g t", t=2)[:, :, 1]
                pool.tensor_tensor(ve[n][:, :], var, eps_col[:, 0:1].to_broadcast([P, count]), ALU.add)\
                    .then_inc(ve_done[n], count)

            def power(slot, n, lag, count=1):
                slot.wait(pool, ve_done[n], lag)
                pool.tensor_tensor(rs[n][:, slot.buf(lag, 2) if count == 1 else 0, :], ve[n][:, :],
                                   half_neg[:, 0:1].to_broadcast([P, count]), ALU.pow)\
                    .then_inc(rs_done[n], count)

            def low_x(slot):
                if slot.on(L_EDGE):
                    slot.wait(pool, x_hi_done, L_EDGE)
                    slot.wait(pool, edge_mm, L_EDGE, 1)
                    pool.tensor_tensor(x_lo[:, :], x_in[:, slot.buf(L_EDGE, 4), :], x_hi[:, :].bitcast(F32),
                                       ALU.subtract).then_inc(x_lo_done, 1)

            def emit(slot):
                if slot.on(L_GCN):
                    slot.wait(pool, x2_done, L_GCN)
                    slot.wait(pool, r2_done, L_GCN, 1)
                    pool.tensor_tensor(x2b[:, :], x2[:, slot.buf(L_GCN, 2), :], bias2[:, :], ALU.add)\
                        .then_inc(x2b_done, 1)
                if slot.on(L_OUT) and slot.part(L_OUT) == GROUP - 1:
                    inv_std(slot, "3", L_OUT, GROUP)
                    mean = mv["3"][:, 0, :].rearrange("p (g t) -> p g t", t=2)[:, :, 0]
                    slot.wait(pool, mv_done["3"], L_OUT)
                    pool.tensor_tensor(neg_mean[:, :], mean, neg_one[:, 0:1].to_broadcast([P, GROUP]),
                                       ALU.mult).then_inc(neg_mean_done, GROUP)
                    slot.wait(pool, neg_mean_done, L_OUT)
                    slot.wait(pool, rs_done["3"], L_OUT)
                    slot.wait(pool, out_done, L_OUT, GROUP)
                    pool.tensor_tensor(out_shift[:, :], neg_mean[:, :], rs["3"][:, 0, :], ALU.mult)\
                        .then_inc(out_shift_done, GROUP)
                if slot.on(L_EDGE) and not slot.on(L_QK):
                    inv_std(slot, "0", L_EDGE)
                if slot.on(L_GAT):
                    slot.wait(pool, e1_done, L_GAT)
                if slot.on(L_EDGE) and slot.on(L_QK):
                    add_eps(slot, "0", L_EDGE)
                if slot.on(L_GAT):
                    b2 = slot.buf(L_GAT, 2)
                    pool.tensor_scalar(e1[:, :], e1[:, :], 1.0, -1.0, ALU.min, ALU.add)\
                        .then_inc(e1m_done, 1)
                if slot.on(L_EDGE) and slot.on(L_QK):
                    power(slot, "0", L_EDGE)
                if slot.on(L_GAT):
                    slot.wait(pool, e1m_done, L_GAT)
                    slot.wait(pool, r1_done, L_GAT)
                    pool.tensor_tensor(r1[:, b2, :], r1[:, b2, :], e1[:, :], ALU.add)\
                        .then_inc(r1_sum_done, 1)
                if slot.on(L_PV):
                    k, first = slot.part(L_PV), slot.buf(L_PV, BUFS) // GROUP * GROUP
                    slot.wait(pool, o_norm_done, L_PV)
                    if k == 0:
                        slot.wait(pool, x4_init, L_PV - (GROUP - 1))
                    res = x4[:, first:first + GROUP, k * CHUNKS * P:(k + 1) * CHUNKS * P]
                    pool.tensor_tensor(res, res, o_norm[:, :, :], ALU.add).then_inc(x4_done, 1)
                if slot.on(L_V):
                    slot.wait(pool, x3_done, L_V)
                    stored = (slot.graph(L_V) - slot.part(L_V) - BUFS) * (16 // GROUP) + 16
                    if not (isinstance(stored, int) and stored <= 0):
                        pool.wait_ge(out_stored[slot.part(L_V)], stored)
                    pool.tensor_tensor(x4[:, slot.buf(L_V, BUFS), :], x3[:, slot.buf(L_V, 2), :],
                                       bv_row[:, :], ALU.add).then_inc(x4_init, 1)
                low_x(Slot(slot.base, slot.offset + 1))
                if slot.on(L_GAT):
                    inv_std(slot, "1", L_GAT)
                if slot.on(L_GCN):
                    inv_std(slot, "2", L_GCN)
                for n in range(len(w_order)):
                    if slot.first(n):
                        split_weight(n)

            pool.wait_ge(const_in, 16 * 6)
            low_x(Slot(0, 0))
            slots(pool, emit)

        @block.scalar
        def _(act):
            def split_weight(n):
                act.wait_ge(w_in[n % 2], 16 * (n // 2 + 1))
                act.activation(weights[w_order[n]][0][:, :, :], stage[n % 2], ACT.Copy).then_inc(w_hi_done, 1)

            act.wait_ge(k_zero, 2)
            act.wait_ge(setup_mm, 1)
            act.activation(adj_t_hi[:, :], att_bank[:, 0:P], ACT.Copy).then_inc(adj_hi_done, 1)
            def biased(dst, src, bias):
                return act.activation(dst, src, ACT.Identity, bias=bias)

            def round_x(slot):
                if slot.on(L_EDGE):
                    b4 = slot.buf(L_EDGE, 4)
                    act.wait_ge(x_loaded[b4], (slot.graph(L_EDGE) - b4) * 4 + 16)
                    slot.wait(act, edge_mm, L_EDGE, 1)
                    slot.wait(act, x_lo_done, L_EDGE, 1)
                    act.activation(x_hi[:, :], x_in[:, b4, :], ACT.Copy).then_inc(x_hi_done, 1)

            def emit(slot):
                if Slot(slot.base, slot.offset - 1).on(L_V):
                    lag = L_V + 1
                    slot.wait(act, v_mm, lag)
                    slot.wait(act, pv_mm, L_PV, 1)
                    act.activation(v_sb[:, slot.buf(lag, BUFS), :], rot[3][:, :], ACT.Copy)\
                        .then_inc(v_done, 1)
                if slot.on(L_QK):
                    slot.wait(act, q_mm, L_QK)
                    slot.wait(act, score_mm, L_QK, 1)
                    for c in range(CHUNKS):
                        chunk = slot.part(L_QK) * CHUNKS + c
                        ins = biased(q_hi[:, c, :], q_bank(c), qb_col[:, chunk:chunk + 1])
                    ins.then_inc(q_hi_done, 1)
                if slot.on(L_GAT):
                    slot.wait(act, z1_mm, L_GAT, 1)
                    slot.wait(act, y1_mm, L_GAT)
                    act.activation(y1_hi[:, :], rot[1][:, :], ACT.Copy).then_inc(y1_hi_done, 1)
                if slot.on(L_ATT):
                    b2, b4 = slot.buf(L_ATT, 2), slot.buf(L_ATT, 4)
                    slot.wait(act, s2_mm, L_ATT)
                    slot.wait(act, lrelu_done, L_ATT, 2)
                    act.activation(z0[:, b2, :], s2_bank[:, 0:P], ACT.Identity,
                                   bias=s1_col[:, b4:b4 + 1]).then_inc(z0_done, 1)
                if slot.on(L_QK):
                    slot.wait(act, k_mm, L_QK)
                    slot.wait(act, score_mm, L_QK, 1)
                    for c in range(CHUNKS):
                        chunk = slot.part(L_QK) * CHUNKS + c
                        for h, rows in enumerate(HEAD_ROWS):
                            ins = biased(k_hi[rows, c, :, h, :], k_bank(c, rows), kb_col[rows, chunk:chunk + 1])
                    ins.then_inc(k_hi_done, 1)
                if slot.on(L_ATT):
                    slot.wait(act, att_nmax_done, L_ATT)
                    slot.wait(act, att_n_done, L_ATT, 2)
                    act.activation(att_p[:, b2, :], att_e[:, b2, :], ACT.Exp, bias=att_nmax[:, b2:b2 + 1],
                                   accum_out=att_sum[:, b2:b2 + 1]).then_inc(att_exp, 1)
                if slot.on(L_PV):
                    slot.wait(act, pt0_mm, L_PV)
                    slot.wait(act, pv_mm, L_PV, 1)
                    act.activation(probs_t[:, 0, :, :].rearrange("p t n -> p (t n)"), rot[3][:, :], ACT.Copy)\
                        .then_inc(pt0_done, 1)
                    slot.wait(act, pt1_mm, L_PV)
                    act.activation(probs_t[:, 1, :, :].rearrange("p t n -> p (t n)"), rot[0][:, :], ACT.Copy)\
                        .then_inc(pt1_done, 1)
                if slot.on(L_GAT):
                    slot.wait(act, z1_mm, L_GAT)
                    slot.wait(act, r1_sum_done, L_GAT, 1)
                    act.activation(e1[:, :], rot[1][:, :], ACT.Exp).then_inc(e1_done, 1)
                if slot.on(L_OUT) and slot.part(L_OUT) == GROUP - 1:
                    slot.wait(act, out_shift_done, L_OUT)
                    first = slot.buf(L_OUT, BUFS) // GROUP * GROUP
                    for g in range(GROUP):
                        act.activation(x4[:, first + g, :], x4[:, first + g, :], ACT.Identity,
                                       bias=out_shift[:, g:g + 1], scale=rs["3"][:, 0, g:g + 1])\
                           .then_inc(out_done, 1)
                if slot.on(L_GCN):
                    slot.wait(act, z2_mm, L_GCN, 1)
                    slot.wait(act, y2_mm, L_GCN)
                    act.activation(y2_hi[:, :], rot[2][:, :], ACT.Copy).then_inc(y2_hi_done, 1)
                if slot.on(L_ATT):
                    slot.wait(act, att_t_mm, L_ATT)
                    slot.wait(act, y1_mm, L_ATT, 2)
                    act.activation(att_t[:, b2, :], att_bank[:, 0:P], ACT.Copy).then_inc(att_t_done, 1)
                if slot.on(L_TR):
                    buf = slot.buf(L_TR, BUFS)
                    slot.wait(act, xt_mm, L_TR)
                    slot.wait(act, k_mm, L_QK)
                    slot.wait(act, v_mm, L_TR, BUFS)
                    act.activation(xt_hi[:, :, buf, :], rot[2][:, :].rearrange("p (k n) -> p k n", k=KC),
                                   ACT.Copy).then_inc(xt_hi_done, 1)
                round_x(Slot(slot.base, slot.offset + 1))
                if slot.on(L_QK):
                    par = slot.buf(L_QK, 2)
                    slot.wait(act, pt1_mm, L_QK, 2)
                    slot.wait(act, inv_done, L_QK, 2)
                    for c in range(CHUNKS):
                        act.wait_ge(score_nmax_done, slot.graph(L_QK) * CHUNKS + c + 1)
                        for t in range(TILES):
                            g, h = divmod(t, 2)
                            i = (g * CHUNKS + c) * 2 + h
                            ins = act.activation(probs[:, par, c, t, :], score_bank[c][:, t * P:(t + 1) * P],
                                                 ACT.Exp, bias=sc_nmax[:, c, t:t + 1], scale=-1.0,
                                                 accum_out=sc_sum[:, par, i:i + 1])
                    ins.then_inc(score_exp, 1)

                for n in range(1, len(w_order)):
                    if slot.first(n - 1):
                        split_weight(n)

            round_x(Slot(0, 0))
            split_weight(0)
            act.wait_ge(const_in, 16 * 6)
            act.wait_ge(setup_mm, 2)
            act.activation(u2[:, :], rot[2][:, :], ACT.Copy).then_inc(u2_done, 1)
            slots(act, emit)

        @block.vector
        def _(dve):
            dve.wait_ge(setup_mm, 1)
            dve.wait_ge(adj_hi_done, 1)
            dve.tensor_copy(adj_t[:, :], att_bank[:, 0:P])
            dve.tensor_tensor(adj_t_lo[:, :], att_bank[:, 0:P], adj_t_hi[:, :].bitcast(F32), ALU.subtract)\
               .then_inc(setup_copied, 1)
            dve.wait_ge(a_in, 16)
            dve.wait_ge(w_in[0], 16)
            for k in range(KC):
                for n in range(2):
                    if k > 0:
                        dve.wait_ge(wa_done, 2 * k + n - 1)
                    dve.tensor_tensor_reduce(out=wa_tmp[:, n, :], in0=stage[0][:, k, :],
                                             in1=a_rows[:, n, :], scale=1.0, scalar=0.0,
                                             op0=ALU.mult, op1=ALU.add,
                                             accum_out=wa_col[:, n * KC + k:n * KC + k + 1])\
                       .then_inc(wa_done, 1)
            dve.wait_ge(const_in, 16 * 6)
            dve.wait_ge(adj_in, 16)
            dve.tensor_scalar(mask[:, :], adj_sb[:, :], 0.0, MASKED, ALU.is_equal, ALU.mult)\
               .then_inc(consts_done, 1)
            dve.tensor_scalar(beta_i[:, :], ident[:, :], beta_col[:, 0:1], None, ALU.mult)\
               .then_inc(consts_done, 1)
            def biased_low(dst, src, bias, high):
                return dve.scalar_tensor_tensor(out=dst, in0=src, scalar=bias, in1=high.bitcast(F32),
                                                op0=ALU.add, op1=ALU.subtract)

            def statistics(n, src, g=0):
                dve.bn_stats(st[n][:, 6 * g:6 * g + 6], src).then_inc(st_done[n], 1)

            def aggregate(n, par, count=1):
                for g in range(count):
                    dve.bn_aggr(mv[n][:, par, 2 * g:2 * g + 2], st[n][:, 6 * g:6 * g + 6])\
                       .then_inc(mv_done[n], 1)

            def dot_products(slot):
                buf = slot.buf(L_EDGE, 4)
                if slot.first(L_EDGE):
                    dve.wait_ge(setup_mm, 2)
                    dve.tensor_copy(u1[:, :], rot[1][:, :]).then_inc(setup_copied, 1)
                    dve.wait_ge(setup_copied, 2)
                    dve.wait_ge(u2_done, 1)
                slot.wait(dve, x1_done, L_EDGE)
                for n, (u, s) in enumerate(((u1, s1_col), (u2, s2_col))):
                    ins = dve.tensor_tensor_reduce(out=dot_tmp[:, n, :], in0=x1[:, buf, :], in1=u[:, :],
                                                   scale=1.0, scalar=0.0, op0=ALU.mult, op1=ALU.add,
                                                   accum_out=s[:, buf:buf + 1])
                ins.then_inc(dots_done, 1)

            def emit(slot):
                last = slot.on(L_OUT) and slot.part(L_OUT) == GROUP - 1
                if last:
                    first = slot.buf(L_OUT, BUFS) // GROUP * GROUP
                    slot.wait(dve, x4_done, L_OUT)
                    for g in range(GROUP):
                        statistics("3", x4[:, first + g, :], g)
                    slot.wait(dve, st_done["3"], L_OUT)
                if slot.on(L_QK):
                    slot.wait(dve, q_hi_done, L_QK)
                    for c in range(CHUNKS):
                        chunk = slot.part(L_QK) * CHUNKS + c
                        ins = biased_low(q_lo[:, c, :], q_bank(c), qb_col[:, chunk:chunk + 1], q_hi[:, c, :])
                    ins.then_inc(q_lo_done, 1)
                if last:
                    aggregate("3", 0, GROUP)
                if slot.on(L_GAT):
                    slot.wait(dve, y1_hi_done, L_GAT)
                    dve.tensor_tensor(y1_lo[:, :], rot[1][:, :], y1_hi[:, :].bitcast(F32), ALU.subtract)\
                        .then_inc(y1_lo_done, 1)
                if slot.on(L_GCN):
                    c2 = slot.buf(L_GCN, 2)
                    slot.wait(dve, rs_done["1"], L_GCN)
                    slot.wait(dve, x2b_done, L_GCN, 2)
                    slot.wait(dve, y2_mm, L_GCN, 2)
                    dve.tensor_scalar(x2[:, c2, :], r1[:, c2, :], mv["1"][:, c2, 0:1], rs["1"][:, c2, 0:1],
                                      ALU.subtract, ALU.mult).then_inc(x2_done, 1)
                if slot.on(L_TR):
                    c2 = slot.buf(L_TR, 2)
                    slot.wait(dve, rs_done["2"], L_TR)
                    slot.wait(dve, xt_mm, L_TR, 2)
                    slot.wait(dve, x4_init, L_TR, 2)
                    dve.tensor_scalar(x3[:, c2, :], r2[:, :], mv["2"][:, c2, 0:1], rs["2"][:, c2, 0:1],
                                      ALU.subtract, ALU.mult).then_inc(x3_done, 1)
                if slot.on(L_ATT):
                    a2 = slot.buf(L_ATT, 2)
                    slot.wait(dve, z0_done, L_ATT)
                    slot.wait(dve, att_exp, L_ATT, 2)
                    dve.scalar_tensor_tensor(out=att_e[:, a2, :], in0=z0[:, a2, :], scalar=SLOPE,
                                             in1=z0[:, a2, :], op0=ALU.mult, op1=ALU.max)\
                        .then_inc(lrelu_done, 1)
                    slot.wait(dve, lrelu_done, L_ATT)
                if slot.on(L_EDGE):
                    b4 = slot.buf(L_EDGE, 4)
                    dve.wait_ge(x_loaded[b4], (slot.graph(L_EDGE) - b4) * 4 + 16)
                    statistics("0", x_in[:, b4, :])
                if slot.on(L_ATT):
                    dve.tensor_tensor_reduce(out=att_e[:, a2, :], in0=att_e[:, a2, :], in1=adj_sb[:, :],
                                             scale=1.0, scalar=-3.0e38, op0=ALU.mult, op1=ALU.max,
                                             accum_out=att_max[:, a2:a2 + 1]).then_inc(att_max_done, 1)
                if slot.on(L_EDGE):
                    slot.wait(dve, st_done["0"], L_EDGE)
                if slot.on(L_ATT):
                    slot.wait(dve, att_max_done, L_ATT)
                    dve.tensor_scalar(att_nmax[:, a2:a2 + 1], att_max[:, a2:a2 + 1], -1.0, None, ALU.mult)\
                        .then_inc(att_nmax_done, 1)
                if slot.on(L_EDGE):
                    aggregate("0", slot.buf(L_EDGE, 2))
                if slot.on(L_QK):
                    slot.wait(dve, k_hi_done, L_QK)
                    for c in range(CHUNKS):
                        chunk = slot.part(L_QK) * CHUNKS + c
                        for h, rows in enumerate(HEAD_ROWS):
                            ins = biased_low(k_lo[rows, c, :, h, :], k_bank(c, rows), kb_col[rows, chunk:chunk + 1],
                                             k_hi[rows, c, :, h, :])
                    ins.then_inc(k_lo_done, 1)
                if slot.on(L_ATT):
                    slot.wait(dve, att_exp, L_ATT)
                    dve.reciprocal(att_inv[:, a2:a2 + 1], att_sum[:, a2:a2 + 1]).then_inc(att_inv_done, 1)
                    slot.wait(dve, att_inv_done, L_ATT)
                    slot.wait(dve, att_t_mm, L_ATT, 2)
                    dve.scalar_tensor_tensor(out=att_n[:, a2, :], in0=att_p[:, a2, :],
                                             scalar=att_inv[:, a2:a2 + 1], in1=beta_i[:, :],
                                             op0=ALU.mult, op1=ALU.add).then_inc(att_n_done, 1)
                if slot.on(L_PV):
                    par = slot.buf(L_PV, 2)
                    slot.wait(dve, score_exp, L_PV)
                    slot.wait(dve, o_norm_done, L_PV, 1)
                    dve.reciprocal(sc_inv[:, :], sc_sum[:, par, :]).then_inc(inv_done, 1)
                if slot.on(L_GAT):
                    g2, g4 = slot.buf(L_GAT, 2), slot.buf(L_GAT, 4)
                    slot.wait(dve, e1_done, L_GAT)
                    slot.wait(dve, x2_done, L_GAT, 2)
                    dve.scalar_tensor_tensor(out=r1[:, g2, :], in0=rot[1][:, :], scalar=0.0,
                                             in1=x1[:, g4, :], op0=ALU.max, op1=ALU.add)\
                        .then_inc(r1_done, 1)
                if slot.on(L_GCN):
                    slot.wait(dve, y2_hi_done, L_GCN)
                    dve.tensor_tensor(y2_lo[:, :], rot[2][:, :], y2_hi[:, :].bitcast(F32), ALU.subtract)\
                        .then_inc(y2_lo_done, 1)
                if slot.on(L_PV):
                    slot.wait(dve, pv_mm, L_PV)
                    slot.wait(dve, inv_done, L_PV)
                    slot.wait(dve, x4_done, L_PV, 1)
                    dve.tensor_tensor(o_norm[:, :, :].rearrange("p g (c d) -> p (g c) d", d=HEAD),
                                      rot[3][:, :].rearrange("p (h d) -> p h d", d=HEAD),
                                      sc_inv[:, :].unsqueeze(2).to_broadcast([P, CHUNKS * TILES, HEAD]),
                                      ALU.mult).then_inc(o_norm_done, 1)
                if slot.on(L_EDGE):
                    slot.wait(dve, edge_mm, L_EDGE)
                    dve.tensor_reduce(edge_max[:, :], rot[0][:, :], axis=AX.X, op=ALU.max)\
                        .then_inc(edge_max_done, 1)
                    slot.wait(dve, edge_max_done, L_EDGE)
                    dve.tensor_scalar(edge_c[:, :], edge_max[:, :], b0_col[:, 0:1], 0.0, ALU.add, ALU.max)\
                        .then_inc(edge_c_done, 1)
                if slot.on(L_EDGE):
                    e2 = slot.buf(L_EDGE, 2)
                    slot.wait(dve, edge_c_done, L_EDGE)
                    slot.wait(dve, mv_done["0"], L_EDGE)
                    dve.tensor_tensor(edge_m[:, :], mv["0"][:, e2, 0:1], edge_c[:, :], ALU.add)\
                        .then_inc(edge_m_done, 1)
                    slot.wait(dve, edge_m_done, L_EDGE)
                    dve.tensor_tensor(edge_d[:, :], edge_c[:, :], edge_m[:, :], ALU.subtract)\
                        .then_inc(edge_d_done, 1)
                if slot.on(L_QK):
                    slot.wait(dve, score_mm, L_QK)
                    slot.wait(dve, score_exp, L_QK, 1)
                if slot.on(L_EDGE):
                    slot.wait(dve, edge_d_done, L_EDGE)
                    slot.wait(dve, rs_done["0"], L_EDGE)
                    slot.wait(dve, y1_mm, L_EDGE, 4)
                    dve.tensor_scalar(x1[:, b4, :], x_in[:, b4, :], edge_d[:, 0:1], rs["0"][:, e2, 0:1],
                                      ALU.add, ALU.mult).then_inc(x1_done, 1)
                if slot.on(L_EDGE) and not slot.on(L_QK):
                    dot_products(slot)
                if slot.on(L_QK):
                    for c in range(CHUNKS):
                        for t in range(TILES):
                            tile = score_bank[c][:, t * P:(t + 1) * P]
                            ins = dve.tensor_tensor_reduce(out=tile, in0=tile, in1=mask[:, :], scale=-SCALE,
                                                           scalar=3.0e38, op0=ALU.add, op1=ALU.min,
                                                           accum_out=sc_nmax[:, c, t:t + 1])
                        ins.then_inc(score_nmax_done, 1)
                if slot.on(L_TR):
                    buf = slot.buf(L_TR, BUFS)
                    slot.wait(dve, xt_hi_done, L_TR)
                    dve.tensor_tensor(xt_lo[:, :, buf, :], rot[2][:, :].rearrange("p (k n) -> p k n", k=KC),
                                      xt_hi[:, :, buf, :].bitcast(F32), ALU.subtract).then_inc(xt_lo_done, 1)
                if slot.on(L_GAT):
                    slot.wait(dve, r1_sum_done, L_GAT)
                    statistics("1", r1[:, g2, :])
                    slot.wait(dve, st_done["1"], L_GAT)
                if slot.on(L_GCN):
                    slot.wait(dve, z2_mm, L_GCN)
                    slot.wait(dve, x2b_done, L_GCN)
                    slot.wait(dve, x3_done, L_GCN, 1)
                    dve.tensor_tensor(r2[:, :], rot[1][:, :], x2b[:, :], ALU.add).then_inc(r2_done, 1)
                if slot.on(L_GAT):
                    aggregate("1", g2)
                if slot.on(L_GCN):
                    slot.wait(dve, r2_done, L_GCN)
                    statistics("2", r2[:, :])
                    slot.wait(dve, st_done["2"], L_GCN)
                if slot.on(L_EDGE) and slot.on(L_QK):
                    dot_products(slot)
                if slot.on(L_GCN):
                    aggregate("2", slot.buf(L_GCN, 2))

            slots(dve, emit)

        @block.tensor
        def _(pe):
            def three(outp, lhs, rhs, first, last):
                (lh, ll), (rh, rl) = lhs, rhs
                pe.matmul(outp, lh, rh, start=first, stop=False)
                pe.matmul(outp, lh, rl, start=False, stop=False)
                return pe.matmul(outp, ll, rh, start=False, stop=last)

            def dense(bank, lhs, w):
                for k in range(KC):
                    ins = three(bank[:, :], [a[:, k, :] for a in lhs], [b[:, k, :] for b in weights[w]],
                                k == 0, k == KC - 1)
                return ins

            pe.wait_ge(ident_done, 1)
            pe.wait_ge(adj_in, 16)
            pe.transpose(att_bank[:, 0:P], adj_sb[:, :], ident[:, :]).then_inc(setup_mm, 1)
            pe.wait_ge(setup_copied, 1)

            def weight_split(slot, w, lag):
                if slot.first(lag):
                    pe.wait_ge(w_lo_done, w_order.index(w) + 1)

            y1 = [a[:, :].rearrange("p (k n) -> p k n", k=KC) for a in (y1_hi, y1_lo)]
            y2 = [a[:, :].rearrange("p (k n) -> p k n", k=KC) for a in (y2_hi, y2_lo)]

            def projection(bank, w, slot):
                first = slot.buf(L_QK, BUFS) // GROUP * GROUP
                for c in range(CHUNKS):
                    chunk = slot.part(L_QK) * CHUNKS + c
                    for k in range(KC):
                        ins = three(bank[:, c * GROUP * P:(c + 1) * GROUP * P],
                                    [a[:, k, chunk * P:(chunk + 1) * P] for a in weights[w]],
                                    [b[:, k, first:first + GROUP, :].rearrange("p g n -> p (g n)") for b in (xt_hi, xt_lo)],
                                    k == 0, k == KC - 1)
                return ins

            def emit(slot):
                if slot.on(L_QK):
                    weight_split(slot, "wk", L_QK)
                    if slot.part(L_QK) == 0:
                        slot.wait(pe, xt_lo_done, L_QK - (GROUP - 1))
                    slot.wait_last(pe, (edge_max_done, L_EDGE, 1), (pt1_done, L_PV, 1))
                    projection(rot[0], "wq", slot).then_inc(q_mm, 1)
                if slot.on(L_ATT):
                    b4 = slot.buf(L_ATT, 4)
                    slot.wait(pe, dots_done, L_ATT)
                    slot.wait(pe, z0_done, L_ATT, 1)
                    pe.transpose(s2_bank[:, 0:P], s2_col[:, b4:b4 + 1].to_broadcast([P, P]), ident[:, :])\
                      .then_inc(s2_mm, 1)
                if slot.on(L_GAT):
                    g2, g4 = slot.buf(L_GAT, 2), slot.buf(L_GAT, 4)
                    slot.wait(pe, att_t_done, L_GAT)
                    if slot.first(L_GAT):
                        pe.wait_ge(setup_copied, 2)
                        pe.wait_ge(u2_done, 1)
                    slot.wait_last(pe, (r2_done, L_GCN, 1), (r1_done, L_GAT, 1))
                    slot.wait(pe, r1_done, L_GAT, 1)
                    for k in range(KC):
                        ins = pe.matmul(rot[1][:, k * P:(k + 1) * P], x1[:, g4, k * P:(k + 1) * P],
                                        att_t[:, g2, :], start=True, stop=True)
                    ins.then_inc(y1_mm, 1)
                if slot.on(L_QK):
                    slot.wait_last(pe, (xt_lo_done, L_TR, 1), (y2_lo_done, L_GCN, 1), (k_lo_done, L_QK, 1))
                    projection(rot[2], "wk", slot).then_inc(k_mm, 1)
                if slot.on(L_PV):
                    par = slot.buf(L_PV, 2)
                    slot.wait(pe, score_exp, L_PV)
                    slot.wait_last(pe, (v_done, L_V, 1), (o_norm_done, L_PV, 1))
                    for t in range(TILES):
                        ins = pe.transpose(rot[3][:, t * P:(t + 1) * P], probs[:, par, 0, t, :], ident[:, :])
                    ins.then_inc(pt0_mm, 1)
                    slot.wait_last(pe, (q_lo_done, L_QK, 0), (pt1_done, L_PV, 1))
                    for t in range(TILES):
                        ins = pe.transpose(rot[0][:, t * P:(t + 1) * P], probs[:, par, 1, t, :], ident[:, :])
                    ins.then_inc(pt1_mm, 1)
                if slot.on(L_GAT):
                    slot.wait(pe, y1_lo_done, L_GAT)
                    weight_split(slot, "w1", L_GAT)
                    dense(rot[1], y1, "w1").then_inc(z1_mm, 1)
                if slot.on(L_PV):
                    slot.wait(pe, pt0_done, L_PV)
                    slot.wait(pe, pt1_done, L_PV)
                    if slot.part(L_PV) == 0:
                        slot.wait(pe, v_done, L_PV - (GROUP - 1))
                    first = slot.buf(L_PV, BUFS) // GROUP * GROUP
                    for g in range(GROUP):
                        for c in range(CHUNKS):
                            for h in range(2):
                                at = ((g * CHUNKS + c) * 2 + h) * HEAD
                                col = (slot.part(L_PV) * CHUNKS + c) * P + h * HEAD
                                ins = pe.matmul(rot[3][:, at:at + HEAD], probs_t[:, c, g * 2 + h, :],
                                                v_sb[:, first + g, col:col + HEAD], start=True, stop=True)
                    ins.then_inc(pv_mm, 1)
                if slot.on(L_GCN):
                    slot.wait(pe, x2_done, L_GCN)
                    slot.wait_last(pe, (k_lo_done, L_QK, 0), (xt_lo_done, L_TR, 1), (y2_lo_done, L_GCN, 1))
                    for k in range(KC):
                        ins = pe.matmul(rot[2][:, k * P:(k + 1) * P], x2[:, slot.buf(L_GCN, 2), k * P:(k + 1) * P],
                                        adj_t[:, :], start=True, stop=True)
                    ins.then_inc(y2_mm, 1)
                if slot.on(L_EDGE):
                    b4 = slot.buf(L_EDGE, 4)
                    slot.wait(pe, x_lo_done, L_EDGE)
                    slot.wait_last(pe, (pt1_done, L_PV, 0), (q_lo_done, L_QK, 0), (edge_max_done, L_EDGE, 1))
                    three(rot[0][:, :], (adj_t_hi[:, :], adj_t_lo[:, :]), (x_hi[:, :], x_lo[:, :]), True, True)\
                        .then_inc(edge_mm, 1)
                    if slot.first(L_EDGE):
                        pe.wait_ge(wa_done, 2 * KC)
                        for n in range(2):
                            for k in range(KC):
                                ins = pe.transpose(rot[1 + n][:, k * P:(k + 1) * P],
                                                   wa_col[:, n * KC + k:n * KC + k + 1].to_broadcast([P, P]), ident[:, :])
                        ins.then_inc(setup_mm, 1)
                if slot.on(L_ATT):
                    slot.wait(pe, att_n_done, L_ATT)
                    slot.wait(pe, att_t_done, L_ATT, 1)
                    pe.transpose(att_bank[:, 0:P], att_n[:, slot.buf(L_ATT, 2), :], ident[:, :])\
                      .then_inc(att_t_mm, 1)
                if slot.on(L_QK):
                    slot.wait(pe, q_lo_done, L_QK)
                    slot.wait(pe, k_lo_done, L_QK)
                    slot.wait(pe, score_exp, L_QK, 1)
                    for c in range(CHUNKS):
                        for g in range(GROUP):
                            ins = three(score_bank[c][:, g * 2 * P:(g + 1) * 2 * P],
                                        [a[:, c, g * P:(g + 1) * P] for a in (q_hi, q_lo)],
                                        [b[:, c, g, :, :].rearrange("p h n -> p (h n)") for b in (k_hi, k_lo)],
                                        True, True)
                    ins.then_inc(score_mm, 1)
                if slot.on(L_TR):
                    slot.wait(pe, x3_done, L_TR)
                    slot.wait_last(pe, (y2_lo_done, L_GCN, 0), (k_lo_done, L_QK, 0), (xt_lo_done, L_TR, 1))
                    for k in range(KC):
                        ins = pe.transpose(rot[2][:, k * P:(k + 1) * P], x3[:, slot.buf(L_TR, 2), k * P:(k + 1) * P],
                                           ident[:, :])
                    ins.then_inc(xt_mm, 1)
                if slot.on(L_GCN):
                    slot.wait(pe, y2_lo_done, L_GCN)
                    weight_split(slot, "w2", L_GCN)
                    slot.wait_last(pe, (r1_done, L_GAT, 0), (r2_done, L_GCN, 1))
                    dense(rot[1], y2, "w2").then_inc(z2_mm, 1)
                if slot.on(L_V):
                    buf = slot.buf(L_V, BUFS)
                    slot.wait(pe, xt_lo_done, L_V)
                    weight_split(slot, "wv", L_V)
                    slot.wait_last(pe, (o_norm_done, L_PV, 0), (v_done, L_V, 1))
                    dense(rot[3], [a[:, :, buf, :] for a in (xt_hi, xt_lo)], "wv").then_inc(v_mm, 1)

            slots(pe, emit)


_INS = ["x", "adj", "L0_gnn_b", "L1_gnn_W", "L1_gnn_a", "L1_gnn_beta", "L2_gnn_weight", "L2_gnn_bias",
        "L3_gnn_Wq", "L3_gnn_bq", "L3_gnn_Wk", "L3_gnn_bk", "L3_gnn_Wv", "L3_gnn_bv"]


def kernel(**inputs):
    import numpy as _np
    import concourse.bacc as _bacc
    from concourse import mybir as _mybir
    from concourse.bass_utils import run_bass_kernel_spmd as _run

    nc = _bacc.Bacc("TRN2", target_bir_lowering=False, num_devices=1)
    arrays, args = {}, []
    for name in _INS:
        a = _np.ascontiguousarray(inputs[name])
        arrays[f"in_{name}"] = a
        args.append(nc.dram_tensor(f"in_{name}", a.shape, _mybir.dt.from_np(a.dtype), kind="ExternalInput").ap())
    args.append(nc.dram_tensor("out_x", (GRAPHS, NODES, FEATS), _mybir.dt.float32, kind="ExternalOutput").ap())
    graph_layers_kernel(nc, *args)
    r = _run(nc, [arrays], core_ids=[0])
    return r.results[0]["out_x"]
```
